# Optimizing a Trainium2 kernel written in Bass

```python
import numpy as np
import jax
import jax.numpy as jnp

def _softmax(x, axis=-1):
    return jax.nn.softmax(x, axis=axis)

def _gelu(x):
    return jax.nn.gelu(x, approximate=True)

def _silu(x):
    return jax.nn.silu(x)

def _sigmoid(x):
    return jax.nn.sigmoid(x)

def _layernorm(x, axis=-1, eps=1e-05):
    m = jnp.mean(x, axis=axis, keepdims=True)
    v = jnp.var(x, axis=axis, keepdims=True)
    return (x - m) / jnp.sqrt(v + eps)

def _scatter_add(tgt, idx, src, axis=0):
    return tgt.at[idx].add(src)

def _segment_sum(src, seg, n):
    return jax.ops.segment_sum(src, seg, n)
kernel_name = 'mk_sandwich_d1_jaxref_r8_123417'

def setup_inputs(seed: int=0):
    np.random.seed(seed)
    _w = jnp.asarray

    def _L0_attn_setup():
        import jax, jax.numpy as jnp
        import numpy as np
        EPS = 1e-08

        def rms_norm_multihead(x, weight):
            x32 = x.astype(jnp.float32)
            normed = x32 * jax.lax.rsqrt(jnp.mean(x32 * x32, axis=-1, keepdims=True) + EPS)
            return normed.astype(x.dtype) * weight
        key = jax.random.key(seed)
        k0, k1, k2 = jax.random.split(key, 3)
        B, L, D, H = (2, 128, 128, 16)
        d = D // H
        X = jax.random.normal(k0, (B, L, D), dtype=jnp.float32)
        Wq = jax.random.normal(k1, (D, D), dtype=jnp.float32) * 0.02
        Wv = jax.random.normal(k2, (D, D), dtype=jnp.float32) * 0.02
        q_norm_w = jnp.ones((H, d), dtype=jnp.float32)
        v_norm_w = jnp.ones((H, d), dtype=jnp.float32)
        return {'X': X, 'Wq': Wq, 'Wv': Wv, 'q_norm_w': q_norm_w, 'v_norm_w': v_norm_w}
    _L0_attn_in = _L0_attn_setup()

    def _L0_ffn_setup():
        import jax, jax.numpy as jnp
        import numpy as np
        DIM = 128
        DEPTH = 6
        HEADS = 16
        DIM_HEAD = 64
        WINDOW = 32
        INNER = HEADS * DIM_HEAD
        DIM_INNER = int(DIM * 4 * 2 / 3)
        QK_SCALE = 8.0

        def shift_tokens(t):
            a, s = jnp.split(t, 2, -1)
            s = jnp.pad(s, ((0, 0), (1, 0), (0, 0)))[:, :-1]
            return jnp.concatenate([a, s], -1)

        def l2norm(t):
            return t / jnp.maximum(jnp.linalg.norm(t, axis=-1, keepdims=True), 1e-12)

        def rotate_half(x):
            x1, x2 = jnp.split(x, 2, -1)
            return jnp.concatenate([-x2, x1], -1)

        def rotary_tables(n):
            half = jnp.arange(0, DIM_HEAD, 2, dtype=jnp.float32)
            inv_freq = 1.0 / 10000.0 ** (half / DIM_HEAD)
            t = jnp.arange(n, dtype=jnp.float32)
            freqs = t[:, None] * inv_freq[None, :]
            freqs = jnp.concatenate([freqs, freqs], -1)
            base_scale = (half + 0.4 * DIM_HEAD) / (1.4 * DIM_HEAD)
            power = (t - n // 2) / (WINDOW // 2)
            scale = base_scale[None, :] ** power[:, None]
            scale = jnp.concatenate([scale, scale], -1)
            return (freqs, scale)

        def local_attention(q, k, v):
            b, h, n, d = q.shape
            w = WINDOW
            nw = n // w
            bq = q.reshape(b, h, nw, w, d)
            bk = k.reshape(b, h, nw, w, d)
            bv = v.reshape(b, h, nw, w, d)

            def look(t):
                p = jnp.pad(t, ((0, 0), (0, 0), (1, 0), (0, 0), (0, 0)))
                return jnp.concatenate([p[:, :, :nw], p[:, :, 1:]], axis=3)
            bk2, bv2 = (look(bk), look(bv))
            seq = jnp.arange(n).reshape(nw, w)
            seq_p = jnp.pad(seq, ((1, 0), (0, 0)), constant_values=-1)
            jt = jnp.concatenate([seq_p[:nw], seq_p[1:]], axis=1)
            it = seq[:, :, None]
            jb = jt[:, None, :]
            mask = (it < jb) | (it > jb + w) | (jb == -1)
            sim = jnp.einsum('bhwie,bhwje->bhwij', bq, bk2) * QK_SCALE
            sim = jnp.where(mask, -jnp.finfo(sim.dtype).max, sim)
            attn = jax.nn.softmax(sim, -1)
            out = jnp.einsum('bhwij,bhwje->bhwie', attn, bv2)
            return out.reshape(b, h, n, d)

        def attn_layer(x, Wqkv, qs, ksc, Wo):
            b, n, _ = x.shape
            qkv = x @ Wqkv
            q, k, v = jnp.split(qkv, 3, -1)
            sh = lambda t: t.reshape(b, n, HEADS, DIM_HEAD).transpose(0, 2, 1, 3)
            q, k, v = (sh(q), sh(k), sh(v))
            q = l2norm(q) * qs
            k = l2norm(k) * ksc
            freqs, scale = rotary_tables(n)
            cos, sin = (jnp.cos(freqs), jnp.sin(freqs))
            q = q * cos * scale + rotate_half(q) * sin * scale
            inv = 1.0 / scale
            k = k * cos * inv + rotate_half(k) * sin * inv
            out = local_attention(q, k, v)
            out = out.transpose(0, 2, 1, 3).reshape(b, n, INNER)
            return out @ Wo

        def ffn_layer(x, g, bln, W1, b1, W2, b2):
            mu = x.mean(-1, keepdims=True)
            var = ((x - mu) ** 2).mean(-1, keepdims=True)
            xn = (x - mu) / jnp.sqrt(var + 1e-05) * g + bln
            hg = xn @ W1 + b1
            a, gate = jnp.split(hg, 2, -1)
            return a * jax.nn.gelu(gate, approximate=False) @ W2 + b2
        key = jax.random.key(seed)
        ks = jax.random.split(key, 8)
        B, N = (2, 256)
        init = lambda k, shape: jax.random.normal(k, shape, jnp.float32) * 0.02
        return {'x': jax.random.normal(ks[0], (B, N, DIM), jnp.float32), 'Wqkv': init(ks[1], (DEPTH, DIM, 3 * INNER)), 'q_scale': jnp.ones((DEPTH, DIM_HEAD), jnp.float32), 'k_scale': jnp.ones((DEPTH, DIM_HEAD), jnp.float32), 'Wo': init(ks[2], (DEPTH, INNER, DIM)), 'ln_g': jnp.ones((DEPTH, DIM), jnp.float32), 'ln_b': jnp.zeros((DEPTH, DIM), jnp.float32), 'W1': init(ks[3], (DEPTH, DIM, 2 * DIM_INNER)), 'b1': jnp.zeros((DEPTH, 2 * DIM_INNER), jnp.float32), 'W2': init(ks[4], (DEPTH, DIM_INNER, DIM)), 'b2': jnp.zeros((DEPTH, DIM), jnp.float32)}
    _L0_ffn_in = _L0_ffn_setup()
    _d = {'L0_attn_X': _L0_attn_in['X'], 'L0_attn_Wq': _L0_attn_in['Wq'], 'L0_attn_Wv': _L0_attn_in['Wv'], 'L0_attn_q_norm_w': _L0_attn_in['q_norm_w'], 'L0_attn_v_norm_w': _L0_attn_in['v_norm_w'], 'L0_ffn_Wqkv': _L0_ffn_in['Wqkv'], 'L0_ffn_q_scale': _L0_ffn_in['q_scale'], 'L0_ffn_k_scale': _L0_ffn_in['k_scale'], 'L0_ffn_Wo': _L0_ffn_in['Wo'], 'L0_ffn_ln_g': _L0_ffn_in['ln_g'], 'L0_ffn_ln_b': _L0_ffn_in['ln_b'], 'L0_ffn_W1': _L0_ffn_in['W1'], 'L0_ffn_b1': _L0_ffn_in['b1'], 'L0_ffn_W2': _L0_ffn_in['W2'], 'L0_ffn_b2': _L0_ffn_in['b2']}
    _x0 = _d['L0_attn_X']
    _d['L0_attn_X'] = jax.random.normal(jax.random.fold_in(jax.random.key(seed), 1), (2, 1024, 128), dtype=_x0.dtype)
    del _x0
    return _d

def reference(L0_attn_X, L0_attn_Wq, L0_attn_Wv, L0_attn_q_norm_w, L0_attn_v_norm_w, L0_ffn_Wqkv, L0_ffn_q_scale, L0_ffn_k_scale, L0_ffn_Wo, L0_ffn_ln_g, L0_ffn_ln_b, L0_ffn_W1, L0_ffn_b1, L0_ffn_W2, L0_ffn_b2):

    def _L0_attn_ref(X, Wq, Wv, q_norm_w, v_norm_w):
        import jax, jax.numpy as jnp
        import numpy as np
        EPS = 1e-08

        def rms_norm_multihead(x, weight):
            x32 = x.astype(jnp.float32)
            normed = x32 * jax.lax.rsqrt(jnp.mean(x32 * x32, axis=-1, keepdims=True) + EPS)
            return normed.astype(x.dtype) * weight
        B, L, D = X.shape
        H, d = q_norm_w.shape
        K = X.reshape(B, L, H, d)
        Q = rms_norm_multihead((X @ Wq.T).reshape(B, L, H, d), q_norm_w)
        V = rms_norm_multihead((X @ Wv.T).reshape(B, L, H, d), v_norm_w)
        W = jnp.cumsum(jnp.einsum('blhd,blhe->blhde', K, V), axis=1)
        out = jnp.einsum('blhd,blhde->blhe', Q, W).reshape(B, L, D)
        return out

    def _L0_ffn_ref(x, Wqkv, q_scale, k_scale, Wo, ln_g, ln_b, W1, b1, W2, b2):
        import jax, jax.numpy as jnp
        import numpy as np
        DIM = 128
        DEPTH = 6
        HEADS = 16
        DIM_HEAD = 64
        WINDOW = 32
        INNER = HEADS * DIM_HEAD
        DIM_INNER = int(DIM * 4 * 2 / 3)
        QK_SCALE = 8.0

        def shift_tokens(t):
            a, s = jnp.split(t, 2, -1)
            s = jnp.pad(s, ((0, 0), (1, 0), (0, 0)))[:, :-1]
            return jnp.concatenate([a, s], -1)

        def l2norm(t):
            return t / jnp.maximum(jnp.linalg.norm(t, axis=-1, keepdims=True), 1e-12)

        def rotate_half(x):
            x1, x2 = jnp.split(x, 2, -1)
            return jnp.concatenate([-x2, x1], -1)

        def rotary_tables(n):
            half = jnp.arange(0, DIM_HEAD, 2, dtype=jnp.float32)
            inv_freq = 1.0 / 10000.0 ** (half / DIM_HEAD)
            t = jnp.arange(n, dtype=jnp.float32)
            freqs = t[:, None] * inv_freq[None, :]
            freqs = jnp.concatenate([freqs, freqs], -1)
            base_scale = (half + 0.4 * DIM_HEAD) / (1.4 * DIM_HEAD)
            power = (t - n // 2) / (WINDOW // 2)
            scale = base_scale[None, :] ** power[:, None]
            scale = jnp.concatenate([scale, scale], -1)
            return (freqs, scale)

        def local_attention(q, k, v):
            b, h, n, d = q.shape
            w = WINDOW
            nw = n // w
            bq = q.reshape(b, h, nw, w, d)
            bk = k.reshape(b, h, nw, w, d)
            bv = v.reshape(b, h, nw, w, d)

            def look(t):
                p = jnp.pad(t, ((0, 0), (0, 0), (1, 0), (0, 0), (0, 0)))
                return jnp.concatenate([p[:, :, :nw], p[:, :, 1:]], axis=3)
            bk2, bv2 = (look(bk), look(bv))
            seq = jnp.arange(n).reshape(nw, w)
            seq_p = jnp.pad(seq, ((1, 0), (0, 0)), constant_values=-1)
            jt = jnp.concatenate([seq_p[:nw], seq_p[1:]], axis=1)
            it = seq[:, :, None]
            jb = jt[:, None, :]
            mask = (it < jb) | (it > jb + w) | (jb == -1)
            sim = jnp.einsum('bhwie,bhwje->bhwij', bq, bk2) * QK_SCALE
            sim = jnp.where(mask, -jnp.finfo(sim.dtype).max, sim)
            attn = jax.nn.softmax(sim, -1)
            out = jnp.einsum('bhwij,bhwje->bhwie', attn, bv2)
            return out.reshape(b, h, n, d)

        def attn_layer(x, Wqkv, qs, ksc, Wo):
            b, n, _ = x.shape
            qkv = x @ Wqkv
            q, k, v = jnp.split(qkv, 3, -1)
            sh = lambda t: t.reshape(b, n, HEADS, DIM_HEAD).transpose(0, 2, 1, 3)
            q, k, v = (sh(q), sh(k), sh(v))
            q = l2norm(q) * qs
            k = l2norm(k) * ksc
            freqs, scale = rotary_tables(n)
            cos, sin = (jnp.cos(freqs), jnp.sin(freqs))
            q = q * cos * scale + rotate_half(q) * sin * scale
            inv = 1.0 / scale
            k = k * cos * inv + rotate_half(k) * sin * inv
            out = local_attention(q, k, v)
            out = out.transpose(0, 2, 1, 3).reshape(b, n, INNER)
            return out @ Wo

        def ffn_layer(x, g, bln, W1, b1, W2, b2):
            mu = x.mean(-1, keepdims=True)
            var = ((x - mu) ** 2).mean(-1, keepdims=True)
            xn = (x - mu) / jnp.sqrt(var + 1e-05) * g + bln
            hg = xn @ W1 + b1
            a, gate = jnp.split(hg, 2, -1)
            return a * jax.nn.gelu(gate, approximate=False) @ W2 + b2
        for i in range(DEPTH):
            x = attn_layer(shift_tokens(x), Wqkv[i], q_scale[i], k_scale[i], Wo[i]) + x
            x = ffn_layer(shift_tokens(x), ln_g[i], ln_b[i], W1[i], b1[i], W2[i], b2[i]) + x
        return x
    x = L0_attn_X
    x = x + _layernorm(_L0_attn_ref(_layernorm(x, axis=-1), L0_attn_Wq, L0_attn_Wv, L0_attn_q_norm_w, L0_attn_v_norm_w), axis=-1)
    x = x + _layernorm(_L0_ffn_ref(_layernorm(x, axis=-1), L0_ffn_Wqkv, L0_ffn_q_scale, L0_ffn_k_scale, L0_ffn_Wo, L0_ffn_ln_g, L0_ffn_ln_b, L0_ffn_W1, L0_ffn_b1, L0_ffn_W2, L0_ffn_b2), axis=-1)
    return x

_drawn_inputs = setup_inputs


def setup_inputs(seed=0):
    import zlib

    import numpy as np

    out = dict(_drawn_inputs(seed))
    spreads = {'L0_attn_q_norm_w': (1.0, 0.2),
     'L0_attn_v_norm_w': (1.0, 0.2),
     'L0_ffn_q_scale': (1.0, 0.6),
     'L0_ffn_k_scale': (1.0, 0.6),
     'L0_ffn_ln_g': (1.0, 0.6),
     'L0_ffn_ln_b': (0.0, 0.8),
     'L0_ffn_b1': (0.0, 0.8),
     'L0_ffn_b2': (0.0, 0.346)}
    factors = {'L0_ffn_W1': 4.488, 'L0_ffn_W2': 4.424}
    for name, (base, spread) in spreads.items():
        noise = np.random.default_rng([zlib.crc32(name.encode()), seed]).standard_normal(out[name].shape)
        drawn = base * np.exp(spread * noise) if base else spread * noise
        out[name] = jnp.asarray(drawn.astype(out[name].dtype))
    for name, factor in factors.items():
        out[name] = (out[name] * factor).astype(out[name].dtype)
    return out
```

```python
from contextlib import ExitStack

import concourse.bass as bass
from concourse import mybir

ALU = mybir.AluOpType
ACT = mybir.ActivationFunctionType
AX = mybir.AxisListType
F32 = mybir.dt.float32

P = 128
LAYERS = 6
BATCH, SEQ = 2, 1024
BPB = SEQ // P
NB = BATCH * BPB
STEPS = LAYERS * NB
HEADS, DH = 16, 64
INNER = HEADS * DH
FT = INNER // P
WIN = 32
NW = P // WIN
FF = 341
FFT = [(0, 128), (128, 128), (256, FF - 256)]
LH, LD = 16, 8
MASKED = -4e37
SCORE_SCALE = 8.0


def bcast(ap, axis, count):
    wide = ap.unsqueeze(axis)
    shape = list(wide.shape)
    shape[axis] = count
    return wide.broadcast_to(shape)


def build(nc, x_in, wqv_in, lin_w_in, wqkv_in, scales_in, wo_in, w1_in, b1_in, w2_in, cols_in,
          square_in, head_in, window_in, rope_in, out):
    with ExitStack() as ctx:
        def sb(name, shape, stack=ctx):
            return stack.enter_context(nc.sbuf_tensor(name, shape, F32))

        def sem(name, stack=ctx):
            return stack.enter_context(nc.semaphore(name))

        x1 = sb("x1", [P, NB, P])
        xT = sb("xT", [P, NB * P])
        square = sb("square", [P, 4, P])
        minus_half = sb("minus_half", [P, 1])
        ident, mean_w, causal, head_blocks = (square[:, k, :] for k in range(4))
        linear_attention(nc, ctx, x_in, wqv_in, lin_w_in, square_in, head_in, x1, xT, square, minus_half)
        layers(nc, ctx, wqkv_in, scales_in, wo_in, w1_in, b1_in, w2_in, cols_in, window_in, rope_in,
               xT, ident, mean_w, minus_half)
        last_norm(nc, ctx, x1, xT, ident, minus_half, out)


class Norm:

    def __init__(self, nc, ctx, tag):
        def sb(name, shape):
            return ctx.enter_context(nc.sbuf_tensor(f"{tag}_{name}", shape, F32))

        def sem(name):
            return ctx.enter_context(nc.semaphore(f"{tag}_{name}"))
        self.sq, self.mean, self.var, self.rstd = (
            sb("sq", [P, NB, P]), sb("mean", [P, NB]), sb("var", [P, NB]), sb("rstd", [P, NB]))
        self.summed, self.meaned, self.centered = sem("summed"), sem("meaned"), sem("centered")
        self.squared, self.varsum, self.vared = sem("squared"), sem("varsum"), sem("vared")
        self.rooted, self.done = sem("rooted"), sem("done")

    def vector(self, dve, k, src, dst):
        dve.tensor_reduce(self.mean[:, :], src, AX.X, ALU.add).then_inc(self.summed, 1)
        dve.wait_ge(self.summed, k)
        dve.tensor_scalar(self.mean[:, :], self.mean[:, :], 1.0 / P, None, ALU.mult).then_inc(self.meaned, 1)
        dve.wait_ge(self.meaned, k)
        dve.tensor_tensor(dst, src, bcast(self.mean[:, :], 2, P), ALU.subtract).then_inc(self.centered, 1)
        dve.wait_ge(self.squared, k)
        dve.tensor_reduce(self.var[:, :], self.sq[:, :, :], AX.X, ALU.add).then_inc(self.varsum, 1)
        dve.wait_ge(self.varsum, k)
        dve.tensor_scalar(self.var[:, :], self.var[:, :], 1.0 / P, 1e-5, ALU.mult, ALU.add)\
           .then_inc(self.vared, 1)
        dve.wait_ge(self.vared, k)
        dve.wait_ge(self.rooted, k)
        dve.tensor_tensor(dst, dst, bcast(self.rstd[:, :], 2, P), ALU.mult).then_inc(self.done, 1)

    def scalar(self, act, k, dst):
        act.wait_ge(self.centered, k)
        act.activation(self.sq[:, :, :], dst, ACT.Square).then_inc(self.squared, 1)

    def gpsimd(self, pool, k, minus_half):
        pool.wait_ge(self.vared, k)
        pool.tensor_tensor(self.rstd[:, :], self.var[:, :], minus_half.broadcast_to([P, NB]), ALU.pow)\
            .then_inc(self.rooted, 1)


def linear_attention(nc, outer, x_in, wqv_in, lin_w_in, square_in, head_in, x1, xT, square, minus_half):
    ident, _, causal, head_blocks = (square[:, k, :] for k in range(4))
    HALF = NB // 2
    NH2 = 2 * LH
    with ExitStack() as ctx:
        def sb(name, shape):
            return ctx.enter_context(nc.sbuf_tensor(name, shape, F32))

        def sem(name):
            return ctx.enter_context(nc.semaphore(name))

        x = sb("x", [P, NB, P])
        wqv = sb("wqv", [P, 2 * P])
        lin_w = sb("lin_w", [P, 2 * P])
        head_of = sb("head_of", [P, LH])
        xn = sb("xn", [P, NB, P])
        xnT = sb("xnT", [P, NB * P])
        qv = sb("qv", [P, NB, 2 * P])
        qvsq = sb("qvsq", [P, HALF, 2 * P])
        qvss = sb("qvss", [P, HALF * NH2])
        qvr = sb("qvr", [P, HALF * NH2])
        qT = sb("qT_lin", [P, NB * P])
        o = sb("o", [P, NB, P])
        k_tok = sb("k_tok", [P, 2, P])
        k_feat = sb("k_feat", [P, 2, P])
        q_feat = sb("q_feat", [P, 2, P])
        q_heads = sb("q_heads", [P, 2, LH, P])
        scores = sb("scores_lin", [P, 2, LH, P])
        state = sb("state", [P, P])
        delta = sb("delta", [P, P])
        ps = ctx.enter_context(nc.psum_tensor("ps_lin", [P, 4096], F32))
        psa = ps[:, 0:2048]
        psb = ps[:, 2048:4096]
        ps_out, ps_state = ps[:, 2048:2048 + P], ps[:, 2560:2560 + P]

        x_loaded, w_loaded, c_loaded = sem("x_loaded"), sem("w_loaded"), sem("c_loaded")
        keysT_done, keysT_copied = sem("keysT_done"), sem("keysT_copied")
        qv_done, qv_squared, qv_summed = sem("qv_done"), sem("qv_squared"), sem("qv_summed")
        qv_meaned, qv_rooted, qv_scaled, qv_weighted = (
            sem("qv_meaned"), sem("qv_rooted"), sem("qv_scaled"), sem("qv_weighted"))
        qsT_done, qsT_copied = sem("qsT_done"), sem("qsT_copied")
        staged, heads_cut = sem("staged"), sem("heads_cut")
        scored, causal_cut = sem("scored"), sem("causal_cut")
        out_done, out_copied, state_done = sem("out_done"), sem("out_copied"), sem("state_done")
        delta_cut, state_kept = sem("delta_cut"), sem("state_kept")
        x1_summed, xT_done, half_set = sem("x1_summed"), sem("xT_done"), sem("half_set")
        norm = Norm(nc, ctx, "ln")
        block = ctx.enter_context(nc.Block())

        @block.sync
        def _(sp):
            sp.dma_start(x[:, :, :], x_in.rearrange("(n p) d -> p n d", p=P)).then_inc(x_loaded, 16)
            sp.dma_start(square[:, :, :], square_in).then_inc(c_loaded, 16)
            sp.dma_start(head_of[:, :], head_in).then_inc(c_loaded, 16)
            sp.dma_start(wqv[:, :], wqv_in).then_inc(w_loaded, 16)
            sp.dma_start(lin_w[:, :], lin_w_in.partition_broadcast(P)).then_inc(w_loaded, 16)

        @block.tensor
        def _(pe):
            pe.wait_ge(c_loaded, 32)
            pe.wait_ge(norm.done, 1)
            for n in range(NB):
                last = pe.transpose(psa[:, n * P:(n + 1) * P], xn[:, n, :], ident)
            last.then_inc(keysT_done, 1)
            pe.wait_ge(w_loaded, 32)
            pe.wait_ge(keysT_copied, 1)
            for g, dst in enumerate((psb, psa)):
                for n in range(HALF):
                    last = pe.matmul(dst[:, n * 2 * P:(n + 1) * 2 * P],
                                     xnT[:, (g * HALF + n) * P:(g * HALF + n + 1) * P], wqv[:, :],
                                     start=True, stop=True)
                last.then_inc(qv_done, 1)
            pe.wait_ge(qv_weighted, 2)
            for n in range(NB):
                last = pe.transpose(psa[:, n * P:(n + 1) * P], qv[:, n, 0:P], ident)
            last.then_inc(qsT_done, 1)
            pe.wait_ge(qsT_copied, 1)

            def score(n, u):
                pe.wait_ge(staged, n + 1)
                pe.wait_ge(heads_cut, n + 1)
                for g in range(4):
                    last = pe.matmul(psa[:, g * 512:(g + 1) * 512], k_feat[:, u, :],
                                     q_heads[:, u, 4 * g:4 * g + 4, :], start=True, stop=True)
                last.then_inc(scored, 1)

            def outputs(n, u):
                pe.wait_ge(state_kept, n + 1)
                pe.matmul(ps_out, q_feat[:, u, :], state[:, :], start=True, stop=False,
                          skip_group_check=True)
                for h in range(LH):
                    v = qv[:, bass.ds(n, 1), P + LD * h:P + LD * (h + 1)]
                    last = pe.matmul(ps_out[:, LD * h:LD * (h + 1)], scores[:, u, h, :], v,
                                     start=False, stop=(h == LH - 1), skip_group_check=True)
                last.then_inc(out_done, 1)
                pe.matmul(ps_state, k_tok[:, u, :], qv[:, bass.ds(n, 1), P:2 * P], start=True, stop=True)\
                  .then_inc(state_done, 1)

            score(0, 0)

            def pair(i, last=False):
                for u in range(2):
                    pe.wait_ge(causal_cut, i + u + 1)
                    if last and u:
                        pe.wait_ge(out_copied, NB - 1)
                    else:
                        score(i + u + 1, 1 - u)
                    outputs(i + u, u)

            with pe.Fori(0, NB // 2 - 1) as j:
                pair(2 * j)
            pair(NB - 2, last=True)
            pe.wait_ge(norm.done, 3)
            for n in range(NB):
                last = pe.transpose(psa[:, n * P:(n + 1) * P], o[:, n, :], ident)
            last.then_inc(xT_done, 1)

        @block.scalar
        def _(act):
            norm.scalar(act, 1, xn[:, :, :])
            act.wait_ge(keysT_done, 1)
            act.activation(xnT[:, :], psa, ACT.Copy).then_inc(keysT_copied, 1)
            for g, src in enumerate((psb, psa)):
                act.wait_ge(qv_done, g + 1)
                act.wait_ge(qv_summed, g) if g else None
                act.activation(qvsq[:, :, :], src.rearrange("p (n d) -> p n d", n=HALF), ACT.Square)\
                   .then_inc(qv_squared, 1)
            act.wait_ge(qsT_done, 1)
            act.activation(qT[:, :], psa, ACT.Copy).then_inc(qsT_copied, 1)

            def stage(n, u):
                act.activation(k_feat[:, u, :], xnT[:, bass.ds(n * P, P)], ACT.Copy)
                act.activation(q_feat[:, u, :], qT[:, bass.ds(n * P, P)], ACT.Copy)
                act.activation(k_tok[:, u, :], xn[:, bass.ds(n, 1), :].rearrange("p a d -> p (a d)"), ACT.Copy)\
                   .then_inc(staged, 1)

            act.wait_ge(qsT_copied, 1)
            act.wait_ge(keysT_copied, 1)
            stage(0, 0)
            stage(1, 1)

            def pair(i, last=False):
                for u in range(2):
                    n = i + u
                    act.wait_ge(out_done, n + 1)
                    act.activation(o[:, bass.ds(n, 1), :].rearrange("p a d -> p (a d)"), ps_out, ACT.Copy)\
                       .then_inc(out_copied, 1)
                    if not last:
                        act.wait_ge(state_done, n + 1)
                        stage(n + 2, u)

            with act.Fori(0, NB // 2 - 1) as j:
                pair(2 * j)
            pair(NB - 2, last=True)
            norm.scalar(act, 2, o[:, :, :])
            norm.scalar(act, 3, o[:, :, :])
            act.wait_ge(xT_done, 1)
            act.activation(xT[:, :], psa, ACT.Copy)

        @block.vector
        def _(dve):
            dve.wait_ge(x_loaded, 16)
            norm.vector(dve, 1, x[:, :, :], xn[:, :, :])
            for g, src in enumerate((psb, psa)):
                dve.wait_ge(qv_squared, g + 1)
                dve.tensor_reduce(qvss[:, :], qvsq[:, :, :].rearrange("p n (h d) -> p (n h) d", d=LD),
                                  AX.X, ALU.add).then_inc(qv_summed, 1)
                dve.wait_ge(qv_summed, g + 1)
                dve.tensor_scalar(qvss[:, :], qvss[:, :], 1.0 / LD, 1e-8, ALU.mult, ALU.add)\
                   .then_inc(qv_meaned, 1)
                dve.wait_ge(qv_rooted, g + 1)
                dst = qv[:, g * HALF:(g + 1) * HALF, :].rearrange("p n (h d) -> p (n h) d", d=LD)
                dve.tensor_tensor(dst, src.rearrange("p (m d) -> p m d", d=LD), bcast(qvr[:, :], 2, LD),
                                  ALU.mult).then_inc(qv_scaled, 1)
            dve.wait_ge(c_loaded, 32)

            def cut_heads(n, u):
                src = qT[:, bass.ds(n * P, P)]
                dve.tensor_tensor(q_heads[:, u, :, :], bcast(src, 1, LH), bcast(head_of[:, :], 2, P),
                                  ALU.mult).then_inc(heads_cut, 1)

            dve.wait_ge(qsT_copied, 1)
            cut_heads(0, 0)

            def step(n, u, last=False):
                if not last:
                    cut_heads(n + 1, 1 - u)
                dve.wait_ge(scored, n + 1)
                dve.tensor_tensor(scores[:, u, :, :], psa.rearrange("p (h q) -> p h q", h=LH),
                                  bcast(causal, 1, LH), ALU.mult).then_inc(causal_cut, 1)
                dve.wait_ge(state_done, n + 1)
                dve.tensor_tensor(delta[:, :], ps_state, head_blocks, ALU.mult).then_inc(delta_cut, 1)
                dve.wait_ge(delta_cut, n + 1)

            for b in range(BATCH):
                base = b * BPB
                dve.memset(state[:, :], 0.0).then_inc(state_kept, 1)

                def pair(i, last_of_row=False, last=False):
                    for u in range(2):
                        n = i + u
                        step(n, u, last=last and u == 1)
                        if not (last_of_row and u == 1):
                            dve.wait_ge(state_kept, n + 1)
                            dve.tensor_tensor(state[:, :], state[:, :], delta[:, :], ALU.add)\
                               .then_inc(state_kept, 1)

                with dve.Fori(0, BPB // 2 - 1) as j:
                    pair(2 * j + base)
                pair(base + BPB - 2, last_of_row=True, last=(b == BATCH - 1))
            dve.wait_ge(out_copied, NB)
            norm.vector(dve, 2, o[:, :, :], o[:, :, :])
            dve.wait_ge(norm.done, 2)
            dve.tensor_tensor(x1[:, :, :], x[:, :, :], o[:, :, :], ALU.add).then_inc(x1_summed, 1)
            dve.wait_ge(x1_summed, 1)
            norm.vector(dve, 3, x1[:, :, :], o[:, :, :])

        @block.gpsimd
        def _(pool):
            pool.memset(minus_half[:, :], -0.5).then_inc(half_set, 1)
            pool.wait_ge(half_set, 1)
            norm.gpsimd(pool, 1, minus_half[:, :])
            pool.wait_ge(w_loaded, 32)
            for g in range(2):
                pool.wait_ge(qv_meaned, g + 1)
                pool.tensor_tensor(qvr[:, :], qvss[:, :], minus_half[:, :].broadcast_to([P, HALF * NH2]),
                                   ALU.pow).then_inc(qv_rooted, 1)
                pool.wait_ge(qv_scaled, g + 1)
                part = qv[:, g * HALF:(g + 1) * HALF, :]
                pool.tensor_tensor(part, part, bcast(lin_w[:, :], 1, HALF), ALU.mult).then_inc(qv_weighted, 1)
            norm.gpsimd(pool, 2, minus_half[:, :])
            norm.gpsimd(pool, 3, minus_half[:, :])


def layers(nc, outer, wqkv_in, scales_in, wo_in, w1_in, b1_in, w2_in, cols_in, window_in, rope_in,
           xT, ident, mean_w, minus_half):
    with ExitStack() as ctx:
        def sb(name, shape):
            return ctx.enter_context(nc.sbuf_tensor(name, shape, F32))

        def sem(name):
            return ctx.enter_context(nc.semaphore(name))

        def psum(name):
            return ctx.enter_context(nc.psum_tensor(name, [P, 1024], F32))

        wqkv = sb("wqkv", [P, 2, 3 * INNER])
        wo = sb("wo", [P, FT, P])
        w1 = sb("w1", [P, 2 * FF])
        w2 = sb("w2", [P, 3, P])
        b1 = sb("b1", [P, 3, 2 * LAYERS])
        cols = sb("cols", [P, 3, LAYERS])
        window = sb("window", [P, 4, WIN * 2])
        rope = sb("rope", [P, BPB, 4, DH])
        scales = sb("scales", [P, LAYERS, 4, DH])
        table = sb("table", [P, 2 * BPB, 4, DH])
        xs1 = sb("xs1", [P, P + 1])
        carry1 = sb("carry1", [P, BPB + 1])
        squares = sb("squares", [P, 2, INNER])
        ss = sb("ss", [P, 2, HEADS])
        rnorm = sb("rnorm", [P, 2, HEADS])
        rot = sb("rot", [P, 2, HEADS, 2, DH // 2])
        rot_sin = sb("rot_sin", [P, 2, HEADS, 2, DH // 2])
        qT = sb("qT", [P, FT, P])
        kT = sb("kT", [P, 2, FT, 2, WIN + P])
        vtok = sb("vtok", [P, 2, 2, FT, DH])
        vwin = sb("vwin", [P, NW, 2, FT, DH])
        sm = sb("sm", [P, HEADS, 2 * WIN])
        rowmax = sb("rowmax", [P, HEADS])
        probs = sb("probs", [P, HEADS, 2 * WIN])
        rowsum = sb("rowsum", [P, HEADS])
        rinv = sb("rinv", [P, HEADS])
        pT = sb("pT", [P, FT, P])
        attn = sb("attn", [P, HEADS, DH])
        attnT = sb("attnT", [P, FT, P])
        xp = sb("xp", [P, P])
        xs2 = sb("xs2", [P, P + 1])
        carry2 = sb("carry2", [P, BPB + 1])
        xc = sb("xc", [P, P])
        xcsq = sb("xcsq", [P, P])
        var = sb("var", [P, P])
        rstd = sb("rstd", [P, P])
        xhat = sb("xhat", [P, P])
        xn2 = sb("xn2", [P, P])
        gate = sb("gate", [P, 3, P])
        hid = sb("hid", [P, 3, P])
        r0, r1, r2, pm = psum("r0"), psum("r1"), psum("r2"), psum("pm")

        names = (
            "tables_loaded wqkv_loaded wo_loaded w1_loaded w2_loaded v_spread "
            "q_proj k_proj v_proj qT_done kT_done scores_done pT_done vwin_free attnT_done wo_done "
            "mean_done var_done up_done down_done "
            "staged1 carried1 qT_copied kT_copied q_squared k_squared v_copied exped pT_copied attnT_copied "
            "xc_squared gelued "
            "cleared tabled q_turned k_turned q_summed k_summed q_floored k_floored q_rooted k_rooted "
            "masked maxed summed inverted normed residual1 centered var_eps rooted hatted xn2_ready "
            "gated x_ready "
            "cleared_pool shifted2 carried2 max_taken q_added q_scaled k_added k_scaled"
        ).split()
        S = {name: sem(name) for name in names}
        block = ctx.enter_context(nc.Block())

        def slot(n):
            return xT[:, bass.ds((n % NB) * P, P)]

        @block.sync
        def _(sp):
            sp.dma_start(window[:, :, :], window_in).then_inc(S["tables_loaded"], 16)
            sp.dma_start(rope[:, :, :, :], rope_in).then_inc(S["tables_loaded"], 16)
            sp.dma_start(scales[:, :, :, :], scales_in.partition_broadcast(P)).then_inc(S["tables_loaded"], 16)
            sp.dma_start(cols[:, :, :], cols_in).then_inc(S["tables_loaded"], 16)
            for t, (at, rows) in enumerate(FFT):
                sp.dma_start(b1[0:rows, t, :], b1_in[at:at + rows, :]).then_inc(S["tables_loaded"], 16)

            def load_wqkv(layer):
                sp.dma_start(wqkv[:, bass.ds(layer % 2, 1), :], wqkv_in[bass.ds(layer, 1), :, :]
                             .rearrange("a p n -> p a n")).then_inc(S["wqkv_loaded"], 16)

            def load_wo(layer):
                sp.dma_start(wo[:, :, :], wo_in[bass.ds(layer, 1), :, :]
                             .rearrange("a (f p) n -> p (a f) n", p=P)).then_inc(S["wo_loaded"], 16)

            def load_ff(layer):
                sp.dma_start(w1[:, :], w1_in[bass.ds(layer, 1), :, :].rearrange("a p n -> p (a n)"))\
                  .then_inc(S["w1_loaded"], 16)
                for t, (at, rows) in enumerate(FFT):
                    sp.dma_start(w2[0:rows, t, :], w2_in[bass.ds(layer, 1), at:at + rows, :]
                                 .rearrange("a p n -> p (a n)")).then_inc(S["w2_loaded"], 16)

            def spread_v(n, u):
                turn = n + 1 if isinstance(n, int) else sp.snap(n + 1)
                sp.wait_ge(S["v_copied"], turn)
                sp.wait_ge(S["vwin_free"], turn)
                for s in range(2):
                    for w in range(NW):
                        own = vtok[WIN * w:WIN * (w + 1), u, s, :, :]
                        before = vtok[WIN * (w - 1):WIN * w, u, s, :, :] if w else vtok[P - WIN:P, 1 - u, s, :, :]
                        for c, src in enumerate((before, own)):
                            at = DH * s + WIN * c
                            sp.dma_start(vwin[at:at + WIN, w, s, :, :], src).then_inc(S["v_spread"], 16)

            load_wqkv(0)
            load_wo(0)
            load_ff(0)
            sp.wait_ge(S["cleared_pool"], 3)
            spread_v(0, 0)
            with sp.Fori(0, LAYERS - 1) as layer:
                sp.wait_ge(S["v_proj"], NB * layer + 1)
                load_wqkv(layer + 1)
                with sp.Fori(0, NB // 2) as j:
                    for u in range(2):
                        spread_v(layer * NB + 2 * j + u + 1, 1 - u)
                used = sp.snap(NB * (layer + 1))
                sp.wait_ge(S["wo_done"], used)
                load_wo(layer + 1)
                sp.wait_ge(S["down_done"], used)
                load_ff(layer + 1)
            with sp.Fori((STEPS - NB) // 2, STEPS // 2 - 1) as j:
                spread_v(2 * j + 1, 1)
                spread_v(2 * j + 2, 0)
            spread_v(STEPS - 1, 1)

        @block.tensor
        def _(pe):
            def project(n):
                pe.wait_ge(S["staged1"], n + 1)
                pe.wait_ge(S["wqkv_loaded"], 16 * (n // NB + 1))
                par = (n // NB) % 2
                for k, (dst, done) in enumerate(((r0, "q_proj"), (r1, "k_proj"), (r2, "v_proj"))):
                    if k == 2 and not (isinstance(n, int) and n == 0):
                        pe.wait_ge(S["masked"], n)
                    for c in range(2):
                        w = wqkv[:, bass.ds(par, 1), k * INNER + c * 512:k * INNER + (c + 1) * 512]
                        last = pe.matmul(dst[:, c * 512:(c + 1) * 512], xs1[:, 0:P],
                                         w.rearrange("p a n -> p (a n)"), start=True, stop=True)
                    last.then_inc(S[done], 1)

            def transpose_all(dst, src, done):
                for f in range(FT):
                    last = pe.transpose(dst[:, f * P:(f + 1) * P], src[:, f * P:(f + 1) * P], ident)
                last.then_inc(S[done], 1)

            def transpose_qk(n):
                pe.wait_ge(S["q_scaled"], n + 1)
                transpose_all(r0, rot[:, 0, :, :, :].rearrange("p h a d -> p (h a d)"), "qT_done")
                pe.wait_ge(S["k_scaled"], n + 1)
                transpose_all(r1, rot[:, 1, :, :, :].rearrange("p h a d -> p (h a d)"), "kT_done")

            def score(n, u):
                pe.wait_ge(S["qT_copied"], n + 1)
                pe.wait_ge(S["kT_copied"], n + 1)
                for f in range(FT):
                    for w in range(NW):
                        rows = slice(WIN * w, WIN * (w + 1))
                        last = pe.matmul(r2[rows, f * P:(f + 1) * P], qT[:, f, rows],
                                         kT[:, u, f, :, WIN * w:WIN * (w + 2)], start=True, stop=True,
                                         tile_position=(0, WIN * w))
                last.then_inc(S["scores_done"], 1)

            def transpose_probs(n, follow):
                pe.wait_ge(S["exped"], n + 1)
                if follow:
                    pe.wait_ge(S["q_squared"], n + 2)
                    pe.wait_ge(S["q_turned"], 3 * (n + 2))
                transpose_all(r0, probs[:, :, :].rearrange("p h k -> p (h k)"), "pT_done")

            def attend(n, follow):
                pe.wait_ge(S["pT_copied"], n + 1)
                pe.wait_ge(S["v_spread"], 16 * 4 * NW * (n + 1))
                if follow:
                    pe.wait_ge(S["k_squared"], n + 2)
                    pe.wait_ge(S["k_turned"], 3 * (n + 2))
                for f in range(FT):
                    for w in range(NW):
                        rows = slice(WIN * w, WIN * (w + 1))
                        last = pe.matmul(r1[rows, f * P:(f + 1) * P], pT[:, f, rows], vwin[:, w, :, f, :],
                                         start=True, stop=True, tile_position=(0, WIN * w))
                last.then_inc(S["vwin_free"], 1)

            def out_project(n, follow):
                pe.wait_ge(S["normed"], n + 1)
                if follow:
                    pe.wait_ge(S["v_copied"], n + 2)
                transpose_all(r2, attn[:, :, :].rearrange("p h d -> p (h d)"), "attnT_done")
                pe.wait_ge(S["attnT_copied"], n + 1)
                pe.wait_ge(S["wo_loaded"], 16 * (n // NB + 1))
                for f in range(FT):
                    last = pe.matmul(pm[:, 512:512 + P], wo[:, f, :], attnT[:, f, :], start=(f == 0),
                                     stop=(f == FT - 1))
                last.then_inc(S["wo_done"], 1)

            def ff_mean(n):
                pe.wait_ge(S["shifted2"], n + 1)
                pe.matmul(pm[:, 0:P], mean_w, xs2[:, 0:P], start=True, stop=True).then_inc(S["mean_done"], 1)

            def ff_var(n):
                pe.wait_ge(S["xc_squared"], n + 1)
                pe.matmul(pm[:, 512:512 + P], mean_w, xcsq[:, :], start=True, stop=True)\
                  .then_inc(S["var_done"], 1)

            def ff_up(n):
                pe.wait_ge(S["xn2_ready"], n + 1)
                pe.wait_ge(S["w1_loaded"], 16 * (n // NB + 1))
                for half in range(2):
                    for t, (at, rows) in enumerate(FFT):
                        last = pe.matmul(pm[0:rows, 512 * half + t * P:512 * half + (t + 1) * P],
                                         w1[:, half * FF + at:half * FF + at + rows], xn2[:, :],
                                         start=True, stop=True)
                last.then_inc(S["up_done"], 1)

            def ff_down(n):
                pe.wait_ge(S["gated"], 3 * (n + 1))
                pe.wait_ge(S["w2_loaded"], 48 * (n // NB + 1))
                for t, (at, rows) in enumerate(FFT):
                    last = pe.matmul(pm[:, 0:P], w2[0:rows, t, :], hid[0:rows, t, :], start=(t == 0),
                                     stop=(t == 2))
                last.then_inc(S["down_done"], 1)

            def step(n, u, first=False, last=False):
                transpose_qk(n)
                if not first:
                    ff_mean(n - 1)
                score(n, u)
                if not first:
                    ff_var(n - 1)
                if not last:
                    project(n + 1)
                if not first:
                    ff_up(n - 1)
                transpose_probs(n, not last)
                if not first:
                    ff_down(n - 1)
                attend(n, not last)
                out_project(n, not last)

            project(0)
            step(0, 0, first=True)
            step(1, 1)
            with pe.Fori(1, STEPS // 2 - 1) as j:
                step(2 * j, 0)
                step(2 * j + 1, 1)
            step(STEPS - 2, 0)
            step(STEPS - 1, 1, last=True)
            ff_mean(STEPS - 1)
            ff_var(STEPS - 1)
            ff_up(STEPS - 1)
            ff_down(STEPS - 1)

        @block.scalar
        def _(act):
            def stage(n):
                act.wait_ge(S["x_ready"], n + 1)
                if not (isinstance(n, int) and n == 0):
                    act.wait_ge(S["carried1"], n)
                x = slot(n)
                act.activation(xs1[0:64, 0:P], x[0:64, :], ACT.Copy)
                act.activation(xs1[64:P, 1:P + 1], x[64:P, :], ACT.Copy)
                act.activation(xs1[64:P, 0:1], carry1[64:P, bass.ds(n % BPB, 1)], ACT.Copy)\
                   .then_inc(S["staged1"], 1)
                act.activation(carry1[64:P, bass.ds(n % BPB + 1, 1)],
                               xT[64:P, bass.ds((n % NB) * P + P - 1, 1)], ACT.Copy).then_inc(S["carried1"], 1)

            def copy_qk(n, u):
                act.wait_ge(S["qT_done"], n + 1)
                act.activation(qT[:, :, :].rearrange("p f t -> p (f t)"), r0[:, :], ACT.Copy)\
                   .then_inc(S["qT_copied"], 1)
                act.wait_ge(S["kT_done"], n + 1)
                src = r1[:, :].rearrange("p (f t) -> p f t", f=FT)
                for s in range(2):
                    rows = slice(64 * s, 64 * s + 64)
                    act.activation(kT[rows, 1 - u, :, s, 0:WIN], src[rows, :, P - WIN:P], ACT.Copy)
                    last = act.activation(kT[rows, u, :, s, WIN:WIN + P], src[rows, :, :], ACT.Copy)
                last.then_inc(S["kT_copied"], 1)

            def square(n, k, src, proj, done):
                act.wait_ge(S[proj], n + 1)
                act.activation(squares[:, k, :], src[:, :], ACT.Square).then_inc(S[done], 1)

            def copy_v(n, u):
                act.wait_ge(S["v_proj"], n + 1)
                if not (isinstance(n, int) and n == 0):
                    act.wait_ge(S["v_spread"], 16 * 4 * NW * n)
                act.activation(vtok[:, u, :, :, :].rearrange("p s f d -> p f s d"),
                               r2[:, :].rearrange("p (f s d) -> p f s d", f=FT, s=2), ACT.Copy)\
                   .then_inc(S["v_copied"], 1)

            def exp(n):
                act.wait_ge(S["max_taken"], n + 1)
                act.activation(probs[:, :, :], sm[:, :, :], ACT.Exp, scale=SCORE_SCALE)\
                   .then_inc(S["exped"], 1)

            def copy_out(src, dst, waits, done, n):
                act.wait_ge(S[waits], n + 1)
                act.activation(dst[:, :, :].rearrange("p f t -> p (f t)"), src[:, :], ACT.Copy)\
                   .then_inc(S[done], 1)

            def ff_square(n):
                act.wait_ge(S["centered"], n + 1)
                act.activation(xcsq[:, :], xc[:, :], ACT.Square).then_inc(S["xc_squared"], 1)

            def ff_gelu(n):
                act.wait_ge(S["up_done"], n + 1)
                for t, (at, rows) in enumerate(FFT):
                    last = act.activation(gate[0:rows, t, :], pm[0:rows, 512 + t * P:512 + (t + 1) * P],
                                          ACT.Gelu, bias=b1[0:rows, t, bass.ds(2 * (n // NB) + 1, 1)])
                last.then_inc(S["gelued"], 1)

            def step(n, u, first=False, last=False):
                copy_qk(n, u)
                if not last:
                    stage(n + 1)
                if not first:
                    ff_square(n - 1)
                if not last:
                    square(n + 1, 0, r0, "q_proj", "q_squared")
                exp(n)
                if not last:
                    square(n + 1, 1, r1, "k_proj", "k_squared")
                    copy_v(n + 1, 1 - u)
                if not first:
                    ff_gelu(n - 1)
                copy_out(r0, pT, "pT_done", "pT_copied", n)
                copy_out(r2, attnT, "attnT_done", "attnT_copied", n)

            act.wait_ge(S["tables_loaded"], 7 * 16)
            act.wait_ge(S["cleared_pool"], 3)
            act.wait_ge(S["cleared"], 1)
            stage(0)
            square(0, 0, r0, "q_proj", "q_squared")
            square(0, 1, r1, "k_proj", "k_squared")
            copy_v(0, 0)
            step(0, 0, first=True)
            step(1, 1)
            with act.Fori(1, STEPS // 2 - 1) as j:
                step(2 * j, 0)
                step(2 * j + 1, 1)
            step(STEPS - 2, 0)
            step(STEPS - 1, 1, last=True)
            ff_square(STEPS - 1)
            ff_gelu(STEPS - 1)

        @block.vector
        def _(dve):
            def tables(entry, layer, parity):
                dve.tensor_tensor(table[:, bass.ds(parity * BPB + entry, 1), :, :]
                                  .rearrange("p a k d -> p (a k d)"),
                                  rope[:, bass.ds(entry, 1), :, :].rearrange("p a k d -> p (a k d)"),
                                  scales[:, bass.ds(layer, 1), :, :].rearrange("p a k d -> p (a k d)"),
                                  ALU.mult).then_inc(S["tabled"], 1)

            def turn(n, k, src, turned, squared, summed, floored):
                dve.wait_ge(S[squared], n + 1)
                entry = ((n // NB) % 2) * BPB + n % BPB
                cos = table[:, bass.ds(entry, 1), 2 * k, :].rearrange("p a d -> p (a d)")
                v = src[:, :].rearrange("p (h a d) -> p h a d", h=HEADS, a=2)
                dve.tensor_tensor(rot[:, k, :, :, :].rearrange("p h a d -> p h (a d)"),
                                  src[:, :].rearrange("p (h d) -> p h d", h=HEADS),
                                  bcast(cos, 1, HEADS), ALU.mult).then_inc(S[turned], 1)
                for a in range(2):
                    sin = table[:, bass.ds(entry, 1), 2 * k + 1, 32 * a:32 * a + 32]\
                        .rearrange("p a d -> p (a d)")
                    dve.tensor_tensor(rot_sin[:, k, :, a, :], v[:, :, 1 - a, :], bcast(sin, 1, HEADS),
                                      ALU.mult).then_inc(S[turned], 1)
                dve.tensor_reduce(ss[:, k, :], squares[:, k, :].rearrange("p (h d) -> p h d", h=HEADS),
                                  AX.X, ALU.add).then_inc(S[summed], 1)
                dve.wait_ge(S[summed], n + 1)
                dve.tensor_scalar(ss[:, k, :], ss[:, k, :], 1e-24, None, ALU.max)\
                   .then_inc(S[floored], 1)

            def turn_q(n):
                turn(n, 0, r0, "q_turned", "q_squared", "q_summed", "q_floored")

            def turn_k(n):
                turn(n, 1, r1, "k_turned", "k_squared", "k_summed", "k_floored")

            def mask(n, u):
                dve.wait_ge(S["scores_done"], n + 1)
                m = window[:, bass.ds((n // 2) % 4, 1), :].rearrange("p a k -> p (a k)") if u == 0 \
                    else window[:, 1, :]
                dve.tensor_tensor(sm[:, :, :], r2[:, :].rearrange("p (h k) -> p h k", h=HEADS),
                                  bcast(m, 1, HEADS), ALU.add).then_inc(S["masked"], 1)
                dve.wait_ge(S["masked"], n + 1)
                dve.tensor_reduce(rowmax[:, :], sm[:, :, :], AX.X, ALU.max).then_inc(S["maxed"], 1)

            def sums(n):
                dve.wait_ge(S["exped"], n + 1)
                dve.tensor_reduce(rowsum[:, :], probs[:, :, :], AX.X, ALU.add).then_inc(S["summed"], 1)
                dve.wait_ge(S["summed"], n + 1)
                dve.reciprocal(rinv[:, :], rowsum[:, :]).then_inc(S["inverted"], 1)

            def normalise(n):
                dve.wait_ge(S["vwin_free"], n + 2)
                dve.wait_ge(S["inverted"], n + 1)
                dve.tensor_tensor(attn[:, :, :], r1[:, :].rearrange("p (h d) -> p h d", h=HEADS),
                                  bcast(rinv[:, :], 2, DH), ALU.mult).then_inc(S["normed"], 1)

            def residual1(n):
                dve.wait_ge(S["wo_done"], n + 1)
                y, x = pm[:, 512:512 + P], slot(n)
                dve.tensor_tensor(xs2[0:64, 0:P], y[0:64, :], x[0:64, :], ALU.add)
                dve.tensor_tensor(xs2[64:P, 1:P + 1], y[64:P, :], x[64:P, :], ALU.add)
                if not (isinstance(n, int) and n == 0):
                    dve.wait_ge(S["carried2"], n)
                dve.tensor_copy(xs2[64:P, 0:1], carry2[64:P, bass.ds(n % BPB, 1)]).then_inc(S["shifted2"], 1)
                dve.tensor_tensor(xp[:, :], y, x, ALU.add).then_inc(S["residual1"], 1)
                dve.wait_ge(S["residual1"], n + 1)
                dve.tensor_copy(carry2[64:P, bass.ds(n % BPB + 1, 1)], xp[64:P, P - 1:P])\
                   .then_inc(S["carried2"], 1)

            def center(n):
                dve.wait_ge(S["mean_done"], n + 1)
                dve.wait_ge(S["shifted2"], n + 1)
                dve.tensor_tensor(xc[:, :], xs2[:, 0:P], pm[:, 0:P], ALU.subtract).then_inc(S["centered"], 1)

            def ff_norm(n):
                dve.wait_ge(S["var_done"], n + 1)
                dve.tensor_scalar(var[:, :], pm[:, 512:512 + P], 1e-5, None, ALU.add)\
                   .then_inc(S["var_eps"], 1)
                dve.wait_ge(S["rooted"], n + 1)
                dve.tensor_tensor(xhat[:, :], xc[:, :], rstd[:, :], ALU.mult).then_inc(S["hatted"], 1)
                dve.wait_ge(S["hatted"], n + 1)
                layer = n // NB
                dve.tensor_scalar(xn2[:, :], xhat[:, :], cols[:, 0, bass.ds(layer, 1)],
                                  cols[:, 1, bass.ds(layer, 1)], ALU.mult, ALU.add)\
                   .then_inc(S["xn2_ready"], 1)

            def ff_gate(n):
                dve.wait_ge(S["gelued"], n + 1)
                for t, (at, rows) in enumerate(FFT):
                    dve.scalar_tensor_tensor(out=hid[0:rows, t, :], in0=pm[0:rows, t * P:(t + 1) * P],
                                             scalar=b1[0:rows, t, bass.ds(2 * (n // NB), 1)],
                                             in1=gate[0:rows, t, :], op0=ALU.add, op1=ALU.mult)\
                       .then_inc(S["gated"], 1)

            def residual2(n):
                dve.wait_ge(S["down_done"], n + 1)
                dve.scalar_tensor_tensor(out=slot(n), in0=pm[:, 0:P], scalar=cols[:, 2, bass.ds(n // NB, 1)],
                                         in1=xp[:, :], op0=ALU.add, op1=ALU.add).then_inc(S["x_ready"], 1)

            def step(n, u, first=False, last=False):
                if not first:
                    residual1(n - 1)
                    center(n - 1)
                mask(n, u)
                if u == 0 and not last:
                    tables((n // 2) % BPB, (n // NB + 1) % LAYERS, (n // NB + 1) % 2)
                if not first:
                    ff_norm(n - 1)
                if not last:
                    if u == 1:
                        dve.wait_ge(S["tabled"], BPB + (n + 1) // 2)
                    turn_q(n + 1)
                    turn_k(n + 1)
                if not first:
                    ff_gate(n - 1)
                sums(n)
                if not first:
                    residual2(n - 1)
                normalise(n)

            dve.memset(carry1[:, :], 0.0).then_inc(S["cleared"], 1)
            dve.memset(carry2[:, :], 0.0).then_inc(S["x_ready"], NB)
            dve.wait_ge(S["tables_loaded"], 7 * 16)
            for entry in range(BPB):
                tables(entry, 0, 0)
            dve.wait_ge(S["tabled"], BPB)
            turn_q(0)
            turn_k(0)
            step(0, 0, first=True)
            step(1, 1)
            with dve.Fori(1, STEPS // 2 - 1) as j:
                step(2 * j, 0)
                step(2 * j + 1, 1)
            step(STEPS - 2, 0)
            step(STEPS - 1, 1, last=True)
            n = STEPS - 1
            residual1(n)
            center(n)
            ff_norm(n)
            ff_gate(n)
            residual2(n)

        @block.gpsimd
        def _(pool):
            pool.memset(kT[:, :, :, :, :], 0.0).then_inc(S["cleared_pool"], 1)
            pool.memset(vwin[:, :, :, :, :], 0.0).then_inc(S["vwin_free"], 1)
            pool.memset(vtok[:, :, :, :, :], 0.0).then_inc(S["cleared_pool"], 1)
            pool.memset(xs1[:, :], 0.0).then_inc(S["cleared_pool"], 1)

            def add_scale(n, k, turned, added, floored, rooted, scaled):
                pool.wait_ge(S[turned], 3 * (n + 1))
                r = rot[:, k, :, :, :].rearrange("p h a d -> p h (a d)")
                pool.tensor_tensor(r, r, rot_sin[:, k, :, :, :].rearrange("p h a d -> p h (a d)"), ALU.add)\
                    .then_inc(S[added], 1)
                pool.wait_ge(S[floored], n + 1)
                pool.tensor_tensor(rnorm[:, k, :], ss[:, k, :], minus_half[:, :].broadcast_to([P, HEADS]),
                                   ALU.pow).then_inc(S[rooted], 1)
                pool.wait_ge(S[added], n + 1)
                pool.wait_ge(S[rooted], n + 1)
                pool.tensor_tensor(r, r, bcast(rnorm[:, k, :], 2, DH), ALU.mult).then_inc(S[scaled], 1)

            def add_scale_qk(n):
                add_scale(n, 0, "q_turned", "q_added", "q_floored", "q_rooted", "q_scaled")
                add_scale(n, 1, "k_turned", "k_added", "k_floored", "k_rooted", "k_scaled")

            def root(n):
                pool.wait_ge(S["var_eps"], n + 1)
                pool.tensor_tensor(rstd[:, :], var[:, :], minus_half[:, :].broadcast_to([P, P]), ALU.pow)\
                    .then_inc(S["rooted"], 1)

            def take_max(n):
                pool.wait_ge(S["maxed"], n + 1)
                pool.tensor_tensor(sm[:, :, :], sm[:, :, :], bcast(rowmax[:, :], 2, 2 * WIN), ALU.subtract)\
                    .then_inc(S["max_taken"], 1)

            def step(n, u, first=False, last=False):
                take_max(n)
                if not first:
                    root(n - 1)
                if not last:
                    add_scale_qk(n + 1)

            add_scale_qk(0)
            step(0, 0, first=True)
            step(1, 1)
            with pool.Fori(1, STEPS // 2 - 1) as j:
                step(2 * j, 0)
                step(2 * j + 1, 1)
            step(STEPS - 2, 0)
            step(STEPS - 1, 1, last=True)
            root(STEPS - 1)


def last_norm(nc, outer, x1, xT, ident, minus_half, out):
    with ExitStack() as ctx:
        y = ctx.enter_context(nc.sbuf_tensor("y", [P, NB, P], F32))
        ps = ctx.enter_context(nc.psum_tensor("ps_last", [P, NB * P], F32))
        turned = ctx.enter_context(nc.semaphore("turned"))
        added = ctx.enter_context(nc.semaphore("added"))
        stored = ctx.enter_context(nc.semaphore("stored"))
        norm = Norm(nc, ctx, "ln_last")
        block = ctx.enter_context(nc.Block())

        @block.tensor
        def _(pe):
            for n in range(NB):
                last = pe.transpose(ps[:, n * P:(n + 1) * P], xT[:, n * P:(n + 1) * P], ident)
            last.then_inc(turned, 1)

        @block.scalar
        def _(act):
            norm.scalar(act, 1, y[:, :, :])

        @block.vector
        def _(dve):
            dve.wait_ge(turned, 1)
            norm.vector(dve, 1, ps[:, :].rearrange("p (n d) -> p n d", n=NB), y[:, :, :])
            dve.wait_ge(norm.done, 1)
            dve.tensor_tensor(y[:, :, :], y[:, :, :], x1[:, :, :], ALU.add).then_inc(added, 1)

        @block.gpsimd
        def _(pool):
            norm.gpsimd(pool, 1, minus_half[:, :])

        @block.sync
        def _(sp):
            sp.wait_ge(added, 1)
            sp.dma_start(out.rearrange("(n p) d -> p n d", p=P), y[:, :, :]).then_inc(stored, 16)
            sp.wait_ge(stored, 16)


def _constants(np):
    eye = np.eye(P)
    i = np.arange(P)
    causal = (i[:, None] <= i[None, :]).astype(float)
    blocks = (i[:, None] // LD == i[None, :] // LD).astype(float)
    square = np.stack([eye, np.full((P, P), 1.0 / P), causal, blocks], 1).astype(np.float32)
    head = (i[:, None] // LD == np.arange(LH)[None, :]).astype(np.float32)
    q = (i % WIN)[:, None]
    k = np.arange(2 * WIN)[None, :]
    allowed = (q <= k) & (k <= q + WIN)
    first = allowed & ((i[:, None] >= WIN) | (k >= WIN))
    window = np.where(np.stack([first, allowed, allowed, allowed], 1), 0.0, MASKED).astype(np.float32)
    half = np.arange(0, DH, 2, dtype=np.float32)
    inv_freq = np.float32(1.0) / np.float32(10000.0) ** (half / np.float32(DH))
    t = np.arange(SEQ, dtype=np.float32)
    freqs = t[:, None] * inv_freq[None, :]
    base = (half + np.float32(0.4 * DH)) / np.float32(1.4 * DH)
    power = (t - SEQ // 2) / np.float32(WIN // 2)
    scale = base[None, :] ** power[:, None]
    cos, sin = np.cos(freqs), np.sin(freqs)
    both = lambda a, b: np.concatenate([a, b], -1)
    parts = [both(cos * scale, cos * scale), both(-sin * scale, sin * scale),
             both(cos / scale, cos / scale), both(-sin / scale, sin / scale)]
    rope = np.stack(parts, 1).reshape(BPB, P, 4, DH).transpose(1, 0, 2, 3).astype(np.float32)
    return square, head, window, np.ascontiguousarray(rope)


def kernel(L0_attn_X, L0_attn_Wq, L0_attn_Wv, L0_attn_q_norm_w, L0_attn_v_norm_w, L0_ffn_Wqkv,
           L0_ffn_q_scale, L0_ffn_k_scale, L0_ffn_Wo, L0_ffn_ln_g, L0_ffn_ln_b, L0_ffn_W1, L0_ffn_b1,
           L0_ffn_W2, L0_ffn_b2):
    import numpy as np
    import concourse.bacc as bacc
    from concourse.bass_utils import run_bass_kernel_spmd

    a = np.asarray
    square, head, window, rope = _constants(np)
    qs, ks = a(L0_ffn_q_scale), a(L0_ffn_k_scale)
    laid = {
        "x": a(L0_attn_X).reshape(BATCH * SEQ, P),
        "wqv": np.concatenate([a(L0_attn_Wq).T, a(L0_attn_Wv).T], 1),
        "lin_w": np.concatenate([a(L0_attn_q_norm_w).reshape(-1), a(L0_attn_v_norm_w).reshape(-1)]),
        "wqkv": a(L0_ffn_Wqkv),
        "scales": np.stack([qs, np.roll(qs, DH // 2, 1), ks, np.roll(ks, DH // 2, 1)], 1),
        "wo": a(L0_ffn_Wo),
        "w1": a(L0_ffn_W1),
        "b1": a(L0_ffn_b1).reshape(LAYERS, 2, FF).transpose(2, 0, 1).reshape(FF, 2 * LAYERS),
        "w2": a(L0_ffn_W2),
        "cols": np.stack([a(L0_ffn_ln_g).T, a(L0_ffn_ln_b).T, a(L0_ffn_b2).T], 1),
        "square": square, "head": head, "window": window, "rope": rope,
    }
    laid = {f"in_{name}": np.ascontiguousarray(v) for name, v in laid.items()}
    nc = bacc.Bacc("TRN2", target_bir_lowering=False, num_devices=1)
    args = [nc.dram_tensor(name, v.shape, mybir.dt.from_np(v.dtype), kind="ExternalInput").ap()
            for name, v in laid.items()]
    out = nc.dram_tensor("out_x", (BATCH * SEQ, P), F32, kind="ExternalOutput").ap()
    build(nc, *args, out)
    r = run_bass_kernel_spmd(nc, [laid], core_ids=[0])
    return r.results[0]["out_x"].reshape(BATCH, SEQ, P)
```

```python
from contextlib import ExitStack

import concourse.bass as bass
from concourse import mybir

ALU = mybir.AluOpType
ACT = mybir.ActivationFunctionType
AX = mybir.AxisListType
F32 = mybir.dt.float32

P = 128
LAYERS = 6
BATCH, SEQ = 2, 1024
BPB = SEQ // P
NB = BATCH * BPB
STEPS = LAYERS * NB
HEADS, DH = 16, 64
INNER = HEADS * DH
FT = INNER // P
WIN = 32
NW = P // WIN
FF = 341
FFT = [(0, 128), (128, 128), (256, FF - 256)]
LH, LD = 16, 8
MASKED = -4e37
SCORE_SCALE = 8.0


def bcast(ap, axis, count):
    wide = ap.unsqueeze(axis)
    shape = list(wide.shape)
    shape[axis] = count
    return wide.broadcast_to(shape)


def build(nc, x_in, wqv_in, lin_w_in, wqkv_in, scales_in, wo_in, w1_in, b1_in, w2_in, cols_in,
          square_in, head_in, window_in, rope_in, out):
    with ExitStack() as ctx:
        def sb(name, shape, stack=ctx):
            return stack.enter_context(nc.sbuf_tensor(name, shape, F32))

        def sem(name, stack=ctx):
            return stack.enter_context(nc.semaphore(name))

        x1 = sb("x1", [P, NB, P])
        xT = sb("xT", [P, NB * P])
        square = sb("square", [P, 4, P])
        eps = sb("eps", [P, 2])
        ident, mean_w, causal, head_blocks = (square[:, k, :] for k in range(4))
        linear_attention(nc, ctx, x_in, wqv_in, lin_w_in, square_in, head_in, x1, xT, square, eps)
        layers(nc, ctx, wqkv_in, scales_in, wo_in, w1_in, b1_in, w2_in, cols_in, window_in, rope_in,
               xT, ident, mean_w, eps)
        last_norm(nc, ctx, x1, xT, ident, eps, out)


class Norm:

    def __init__(self, nc, ctx, tag, eps):
        self.eps = eps
        def sb(name, shape):
            return ctx.enter_context(nc.sbuf_tensor(f"{tag}_{name}", shape, F32))

        def sem(name):
            return ctx.enter_context(nc.semaphore(f"{tag}_{name}"))
        self.sq, self.mean, self.var = sb("sq", [P, NB, P]), sb("mean", [P, NB]), sb("var", [P, NB])
        self.std, self.rstd = sb("std", [P, NB]), sb("rstd", [P, NB])
        self.summed, self.meaned, self.centered = sem("summed"), sem("meaned"), sem("centered")
        self.squared, self.varsum, self.rooted = sem("squared"), sem("varsum"), sem("rooted")
        self.inverted, self.done = sem("inverted"), sem("done")

    def vector(self, dve, k, src, dst):
        dve.tensor_reduce(self.mean[:, :], src, AX.X, ALU.add).then_inc(self.summed, 1)
        dve.wait_ge(self.summed, k)
        dve.tensor_scalar(self.mean[:, :], self.mean[:, :], 1.0 / P, None, ALU.mult).then_inc(self.meaned, 1)
        dve.wait_ge(self.meaned, k)
        dve.tensor_tensor(dst, src, bcast(self.mean[:, :], 2, P), ALU.subtract).then_inc(self.centered, 1)
        dve.wait_ge(self.squared, k)
        dve.tensor_reduce(self.var[:, :], self.sq[:, :, :], AX.X, ALU.add).then_inc(self.varsum, 1)
        dve.wait_ge(self.rooted, k)
        dve.reciprocal(self.rstd[:, :], self.std[:, :]).then_inc(self.inverted, 1)
        dve.wait_ge(self.inverted, k)
        dve.tensor_tensor(dst, dst, bcast(self.rstd[:, :], 2, P), ALU.mult).then_inc(self.done, 1)

    def scalar(self, act, k, dst):
        act.wait_ge(self.centered, k)
        act.activation(self.sq[:, :, :], dst, ACT.Square).then_inc(self.squared, 1)
        act.wait_ge(self.varsum, k)
        act.activation(self.std[:, :], self.var[:, :], ACT.Sqrt, scale=1.0 / P, bias=self.eps)\
           .then_inc(self.rooted, 1)


def linear_attention(nc, outer, x_in, wqv_in, lin_w_in, square_in, head_in, x1, xT, square, eps):
    ident, _, causal, head_blocks = (square[:, k, :] for k in range(4))
    HALF = NB // 2
    NH2 = 2 * LH
    with ExitStack() as ctx:
        def sb(name, shape):
            return ctx.enter_context(nc.sbuf_tensor(name, shape, F32))

        def sem(name):
            return ctx.enter_context(nc.semaphore(name))

        x = sb("x", [P, NB, P])
        wqv = sb("wqv", [P, 2 * P])
        lin_w = sb("lin_w", [P, 2 * P])
        head_of = sb("head_of", [P, LH])
        xn = sb("xn", [P, NB, P])
        xnT = sb("xnT", [P, NB * P])
        qv = sb("qv", [P, NB, 2 * P])
        qvsq = sb("qvsq", [P, HALF, 2 * P])
        qvss = sb("qvss", [P, HALF * NH2])
        qvstd = sb("qvstd", [P, HALF * NH2])
        qvr = sb("qvr", [P, HALF * NH2])
        qT = sb("qT_lin", [P, NB * P])
        o = sb("o", [P, NB, P])
        k_tok = sb("k_tok", [P, 2, P])
        k_feat = sb("k_feat", [P, 2, P])
        q_feat = sb("q_feat", [P, 2, P])
        q_heads = sb("q_heads", [P, 2, LH, P])
        scores = sb("scores_lin", [P, 2, LH, P])
        state = sb("state", [P, P])
        delta = sb("delta", [P, P])
        ps = ctx.enter_context(nc.psum_tensor("ps_lin", [P, 4096], F32))
        psa = ps[:, 0:2048]
        psb = ps[:, 2048:4096]
        ps_out, ps_state = ps[:, 2048:2048 + P], ps[:, 2560:2560 + P]

        x_loaded, w_loaded, c_loaded = sem("x_loaded"), sem("w_loaded"), sem("c_loaded")
        keysT_done, keysT_copied = sem("keysT_done"), sem("keysT_copied")
        qv_done, qv_squared, qv_summed = sem("qv_done"), sem("qv_squared"), sem("qv_summed")
        qv_rooted, qv_inverted, qv_scaled, qv_weighted = (
            sem("qv_rooted"), sem("qv_inverted"), sem("qv_scaled"), sem("qv_weighted"))
        qsT_done, qsT_copied = sem("qsT_done"), sem("qsT_copied")
        staged, heads_cut = sem("staged"), sem("heads_cut")
        scored, causal_cut = sem("scored"), sem("causal_cut")
        out_done, out_copied, state_done = sem("out_done"), sem("out_copied"), sem("state_done")
        delta_cut, state_kept = sem("delta_cut"), sem("state_kept")
        x1_summed, xT_done, eps_set = sem("x1_summed"), sem("xT_done"), sem("eps_set")
        norm = Norm(nc, ctx, "ln", eps[:, 0:1])
        block = ctx.enter_context(nc.Block())

        @block.sync
        def _(sp):
            sp.dma_start(x[:, :, :], x_in.rearrange("(n p) d -> p n d", p=P)).then_inc(x_loaded, 16)
            sp.dma_start(square[:, :, :], square_in).then_inc(c_loaded, 16)
            sp.dma_start(head_of[:, :], head_in).then_inc(c_loaded, 16)
            sp.dma_start(wqv[:, :], wqv_in).then_inc(w_loaded, 16)
            sp.dma_start(lin_w[:, :], lin_w_in.partition_broadcast(P)).then_inc(w_loaded, 16)

        @block.tensor
        def _(pe):
            pe.wait_ge(c_loaded, 32)
            pe.wait_ge(norm.done, 1)
            for n in range(NB):
                last = pe.transpose(psa[:, n * P:(n + 1) * P], xn[:, n, :], ident)
            last.then_inc(keysT_done, 1)
            pe.wait_ge(w_loaded, 32)
            pe.wait_ge(keysT_copied, 1)
            for g, dst in enumerate((psb, psa)):
                for n in range(HALF):
                    last = pe.matmul(dst[:, n * 2 * P:(n + 1) * 2 * P],
                                     xnT[:, (g * HALF + n) * P:(g * HALF + n + 1) * P], wqv[:, :],
                                     start=True, stop=True)
                last.then_inc(qv_done, 1)
            pe.wait_ge(qv_weighted, 2)
            for n in range(NB):
                last = pe.transpose(psa[:, n * P:(n + 1) * P], qv[:, n, 0:P], ident)
            last.then_inc(qsT_done, 1)
            pe.wait_ge(qsT_copied, 1)

            def score(n, u):
                pe.wait_ge(staged, n + 1)
                pe.wait_ge(heads_cut, n + 1)
                for g in range(4):
                    last = pe.matmul(psa[:, g * 512:(g + 1) * 512], k_feat[:, u, :],
                                     q_heads[:, u, 4 * g:4 * g + 4, :], start=True, stop=True)
                last.then_inc(scored, 1)

            def outputs(n, u):
                pe.wait_ge(state_kept, n + 1)
                pe.matmul(ps_out, q_feat[:, u, :], state[:, :], start=True, stop=False,
                          skip_group_check=True)
                for h in range(LH):
                    v = qv[:, bass.ds(n, 1), P + LD * h:P + LD * (h + 1)]
                    last = pe.matmul(ps_out[:, LD * h:LD * (h + 1)], scores[:, u, h, :], v,
                                     start=False, stop=(h == LH - 1), skip_group_check=True)
                last.then_inc(out_done, 1)
                pe.matmul(ps_state, k_tok[:, u, :], qv[:, bass.ds(n, 1), P:2 * P], start=True, stop=True)\
                  .then_inc(state_done, 1)

            score(0, 0)

            def pair(i, last=False):
                for u in range(2):
                    pe.wait_ge(causal_cut, i + u + 1)
                    if last and u:
                        pe.wait_ge(out_copied, NB - 1)
                    else:
                        score(i + u + 1, 1 - u)
                    outputs(i + u, u)

            with pe.Fori(0, NB // 2 - 1) as j:
                pair(2 * j)
            pair(NB - 2, last=True)
            pe.wait_ge(norm.done, 3)
            for n in range(NB):
                last = pe.transpose(psa[:, n * P:(n + 1) * P], o[:, n, :], ident)
            last.then_inc(xT_done, 1)

        @block.scalar
        def _(act):
            act.wait_ge(eps_set, 2)
            norm.scalar(act, 1, xn[:, :, :])
            act.wait_ge(keysT_done, 1)
            act.activation(xnT[:, :], psa, ACT.Copy).then_inc(keysT_copied, 1)
            for g, src in enumerate((psb, psa)):
                act.wait_ge(qv_done, g + 1)
                act.activation(qvsq[:, :, :], src.rearrange("p (n d) -> p n d", n=HALF), ACT.Square)\
                   .then_inc(qv_squared, 1)
                act.wait_ge(qv_summed, g + 1)
                act.activation(qvstd[:, :], qvss[:, :], ACT.Sqrt, scale=1.0 / LD, bias=eps[:, 1:2])\
                   .then_inc(qv_rooted, 1)
            act.wait_ge(qsT_done, 1)
            act.activation(qT[:, :], psa, ACT.Copy).then_inc(qsT_copied, 1)

            def stage(n, u):
                act.activation(k_feat[:, u, :], xnT[:, bass.ds(n * P, P)], ACT.Copy)
                act.activation(q_feat[:, u, :], qT[:, bass.ds(n * P, P)], ACT.Copy)
                act.activation(k_tok[:, u, :], xn[:, bass.ds(n, 1), :].rearrange("p a d -> p (a d)"), ACT.Copy)\
                   .then_inc(staged, 1)

            act.wait_ge(qsT_copied, 1)
            act.wait_ge(keysT_copied, 1)
            stage(0, 0)
            stage(1, 1)

            def pair(i, last=False):
                for u in range(2):
                    n = i + u
                    act.wait_ge(out_done, n + 1)
                    act.activation(o[:, bass.ds(n, 1), :].rearrange("p a d -> p (a d)"), ps_out, ACT.Copy)\
                       .then_inc(out_copied, 1)
                    if not last:
                        act.wait_ge(state_done, n + 1)
                        stage(n + 2, u)

            with act.Fori(0, NB // 2 - 1) as j:
                pair(2 * j)
            pair(NB - 2, last=True)
            norm.scalar(act, 2, o[:, :, :])
            norm.scalar(act, 3, o[:, :, :])
            act.wait_ge(xT_done, 1)
            act.activation(xT[:, :], psa, ACT.Copy)

        @block.vector
        def _(dve):
            dve.wait_ge(x_loaded, 16)
            norm.vector(dve, 1, x[:, :, :], xn[:, :, :])
            for g, src in enumerate((psb, psa)):
                dve.wait_ge(qv_squared, g + 1)
                dve.tensor_reduce(qvss[:, :], qvsq[:, :, :].rearrange("p n (h d) -> p (n h) d", d=LD),
                                  AX.X, ALU.add).then_inc(qv_summed, 1)
                dve.wait_ge(qv_rooted, g + 1)
                dve.reciprocal(qvr[:, :], qvstd[:, :]).then_inc(qv_inverted, 1)
                dve.wait_ge(qv_inverted, g + 1)
                dst = qv[:, g * HALF:(g + 1) * HALF, :].rearrange("p n (h d) -> p (n h) d", d=LD)
                dve.tensor_tensor(dst, src.rearrange("p (m d) -> p m d", d=LD), bcast(qvr[:, :], 2, LD),
                                  ALU.mult).then_inc(qv_scaled, 1)
            dve.wait_ge(c_loaded, 32)

            def cut_heads(n, u):
                src = qT[:, bass.ds(n * P, P)]
                dve.tensor_tensor(q_heads[:, u, :, :], bcast(src, 1, LH), bcast(head_of[:, :], 2, P),
                                  ALU.mult).then_inc(heads_cut, 1)

            dve.wait_ge(qsT_copied, 1)
            cut_heads(0, 0)

            def step(n, u, last=False):
                if not last:
                    cut_heads(n + 1, 1 - u)
                dve.wait_ge(scored, n + 1)
                dve.tensor_tensor(scores[:, u, :, :], psa.rearrange("p (h q) -> p h q", h=LH),
                                  bcast(causal, 1, LH), ALU.mult).then_inc(causal_cut, 1)
                dve.wait_ge(state_done, n + 1)
                dve.tensor_tensor(delta[:, :], ps_state, head_blocks, ALU.mult).then_inc(delta_cut, 1)
                dve.wait_ge(delta_cut, n + 1)

            for b in range(BATCH):
                base = b * BPB
                dve.memset(state[:, :], 0.0).then_inc(state_kept, 1)

                def pair(i, last_of_row=False, last=False):
                    for u in range(2):
                        n = i + u
                        step(n, u, last=last and u == 1)
                        if not (last_of_row and u == 1):
                            dve.wait_ge(state_kept, n + 1)
                            dve.tensor_tensor(state[:, :], state[:, :], delta[:, :], ALU.add)\
                               .then_inc(state_kept, 1)

                with dve.Fori(0, BPB // 2 - 1) as j:
                    pair(2 * j + base)
                pair(base + BPB - 2, last_of_row=True, last=(b == BATCH - 1))
            dve.wait_ge(out_copied, NB)
            norm.vector(dve, 2, o[:, :, :], o[:, :, :])
            dve.wait_ge(norm.done, 2)
            dve.tensor_tensor(x1[:, :, :], x[:, :, :], o[:, :, :], ALU.add).then_inc(x1_summed, 1)
            dve.wait_ge(x1_summed, 1)
            norm.vector(dve, 3, x1[:, :, :], o[:, :, :])

        @block.gpsimd
        def _(pool):
            pool.memset(eps[:, 0:1], 1e-5).then_inc(eps_set, 1)
            pool.memset(eps[:, 1:2], 1e-8).then_inc(eps_set, 1)
            pool.wait_ge(w_loaded, 32)
            for g in range(2):
                pool.wait_ge(qv_scaled, g + 1)
                part = qv[:, g * HALF:(g + 1) * HALF, :]
                pool.tensor_tensor(part, part, bcast(lin_w[:, :], 1, HALF), ALU.mult).then_inc(qv_weighted, 1)


def layers(nc, outer, wqkv_in, scales_in, wo_in, w1_in, b1_in, w2_in, cols_in, window_in, rope_in,
           xT, ident, mean_w, eps):
    with ExitStack() as ctx:
        def sb(name, shape):
            return ctx.enter_context(nc.sbuf_tensor(name, shape, F32))

        def sem(name):
            return ctx.enter_context(nc.semaphore(name))

        def psum(name):
            return ctx.enter_context(nc.psum_tensor(name, [P, 1024], F32))

        wqkv = sb("wqkv", [P, 2, 3 * INNER])
        wo = sb("wo", [P, FT, P])
        w1 = sb("w1", [P, 2 * FF])
        w2 = sb("w2", [P, 3, P])
        b1 = sb("b1", [P, 3, 2 * LAYERS])
        cols = sb("cols", [P, 3, LAYERS])
        window = sb("window", [P, 4, WIN * 2])
        rope = sb("rope", [P, BPB, 4, DH])
        scales = sb("scales", [P, LAYERS, 4, DH])
        table = sb("table", [P, 2 * BPB, 4, DH])
        xs1 = sb("xs1", [P, 2, P + 1])
        carry1 = sb("carry1", [P, BPB + 1])
        squares = sb("squares", [P, 2, INNER])
        ss = sb("ss", [P, 2, HEADS])
        norms = sb("norms", [P, 2, HEADS])
        rnorm = sb("rnorm", [P, 2, HEADS])
        rot = sb("rot", [P, 2, 2, HEADS, 2, DH // 2])
        rot_sin = sb("rot_sin", [P, 2, HEADS, 2, DH // 2])
        qT = sb("qT", [P, FT, P])
        kT = sb("kT", [P, 2, FT, 2, WIN + P])
        vtok = sb("vtok", [P, 2, 2, FT, DH])
        vwin = sb("vwin", [P, NW, 2, FT, DH])
        sm = sb("sm", [P, HEADS, 2 * WIN])
        rowmax = sb("rowmax", [P, HEADS])
        probs = sb("probs", [P, HEADS, 2 * WIN])
        rowsum = sb("rowsum", [P, HEADS])
        rinv = sb("rinv", [P, HEADS])
        pT = sb("pT", [P, FT, P])
        attn = sb("attn", [P, HEADS, DH])
        attnT = sb("attnT", [P, FT, P])
        xp = sb("xp", [P, 2, P])
        xs2 = sb("xs2", [P, P + 1])
        carry2 = sb("carry2", [P, BPB + 1])
        xc = sb("xc", [P, P])
        xcsq = sb("xcsq", [P, P])
        std = sb("std", [P, P])
        rstd = sb("rstd", [P, P])
        xhat = sb("xhat", [P, P])
        xn2 = sb("xn2", [P, P])
        gate = sb("gate", [P, 3, P])
        hid = sb("hid", [P, 3, P])
        r0, r1, r2, pm = psum("r0"), psum("r1"), psum("r2"), psum("pm")

        names = (
            "tables_loaded wqkv_loaded wo_loaded w1_loaded w2_loaded v_spread "
            "q_proj k_proj v_proj qT_done kT_done scores_done pT_done vwin_free attnT_done wo_done "
            "mean_done var_done up_done down_done "
            "staged1 carried1 qT_copied kT_copied q_squared k_squared v_copied exped pT_copied attnT_copied "
            "xc_squared gelued qk_rooted std_rooted "
            "cleared tabled q_turned k_turned q_summed k_summed floored rnorm_ready "
            "masked maxed summed inverted normed residual1 shifted2 carried2 centered rstd_ready hatted "
            "xn2_ready gated x_ready "
            "cleared_pool max_taken q_added q_scaled k_added k_scaled"
        ).split()
        S = {name: sem(name) for name in names}
        block = ctx.enter_context(nc.Block())

        def runs(n):
            return not isinstance(n, int) or 0 <= n < STEPS

        def slots(u):
            return (r0, r1, r2) if u == 0 else (r0, r2, r1)

        def run(eng, step):
            for n in range(-2, 2):
                step(n, n % 2)
            with eng.Fori(1, STEPS // 2 - 1) as j:
                step(2 * j, 0)
                step(2 * j + 1, 1)
            for n in range(STEPS - 2, STEPS + 2):
                step(n, n % 2)

        def slot(n):
            return xT[:, bass.ds((n % NB) * P, P)]

        @block.sync
        def _(sp):
            sp.dma_start(window[:, :, :], window_in).then_inc(S["tables_loaded"], 16)
            sp.dma_start(rope[:, :, :, :], rope_in).then_inc(S["tables_loaded"], 16)
            sp.dma_start(scales[:, :, :, :], scales_in.partition_broadcast(P)).then_inc(S["tables_loaded"], 16)
            sp.dma_start(cols[:, :, :], cols_in).then_inc(S["tables_loaded"], 16)
            for t, (at, rows) in enumerate(FFT):
                sp.dma_start(b1[0:rows, t, :], b1_in[at:at + rows, :]).then_inc(S["tables_loaded"], 16)

            def load_wqkv(layer):
                sp.dma_start(wqkv[:, bass.ds(layer % 2, 1), :], wqkv_in[bass.ds(layer, 1), :, :]
                             .rearrange("a p n -> p a n")).then_inc(S["wqkv_loaded"], 16)

            def load_wo(layer):
                sp.dma_start(wo[:, :, :], wo_in[bass.ds(layer, 1), :, :]
                             .rearrange("a (f p) n -> p (a f) n", p=P)).then_inc(S["wo_loaded"], 16)

            def load_w1(layer):
                sp.dma_start(w1[:, :], w1_in[bass.ds(layer, 1), :, :].rearrange("a p n -> p (a n)"))\
                  .then_inc(S["w1_loaded"], 16)

            def load_w2(layer):
                for t, (at, rows) in enumerate(FFT):
                    sp.dma_start(w2[0:rows, t, :], w2_in[bass.ds(layer, 1), at:at + rows, :]
                                 .rearrange("a p n -> p (a n)")).then_inc(S["w2_loaded"], 16)

            def spread_v(n, u):
                turn = n + 1 if isinstance(n, int) else sp.snap(n + 1)
                sp.wait_ge(S["v_copied"], turn)
                sp.wait_ge(S["vwin_free"], turn)
                for s in range(2):
                    for w in range(NW):
                        own = vtok[WIN * w:WIN * (w + 1), u, s, :, :]
                        before = vtok[WIN * (w - 1):WIN * w, u, s, :, :] if w else vtok[P - WIN:P, 1 - u, s, :, :]
                        for c, src in enumerate((before, own)):
                            at = DH * s + WIN * c
                            sp.dma_start(vwin[at:at + WIN, w, s, :, :], src).then_inc(S["v_spread"], 16)

            load_wqkv(0)
            load_wo(0)
            load_w1(0)
            load_w2(0)
            sp.wait_ge(S["cleared_pool"], 3)
            spread_v(0, 0)
            spread_v(1, 1)
            with sp.Fori(0, LAYERS - 1) as layer:
                sp.wait_ge(S["v_proj"], NB * layer + 1)
                load_wqkv(layer + 1)
                with sp.Fori(1, NB // 2) as j:
                    spread_v(layer * NB + 2 * j, 0)
                    spread_v(layer * NB + 2 * j + 1, 1)
                used = sp.snap(NB * (layer + 1))
                spread_v(used, 0)
                sp.wait_ge(S["wo_done"], used)
                load_wo(layer + 1)
                spread_v(used + 1, 1)
                sp.wait_ge(S["up_done"], used)
                load_w1(layer + 1)
                sp.wait_ge(S["down_done"], used)
                load_w2(layer + 1)
            with sp.Fori((STEPS - NB) // 2 + 1, STEPS // 2) as j:
                spread_v(2 * j, 0)
                spread_v(2 * j + 1, 1)

        @block.tensor
        def _(pe):
            def project(n, u, k, dst, done):
                pe.wait_ge(S["staged1"], n + 1)
                pe.wait_ge(S["wqkv_loaded"], 16 * (n // NB + 1))
                for c in range(2):
                    w = wqkv[:, bass.ds((n // NB) % 2, 1), k * INNER + c * 512:k * INNER + (c + 1) * 512]
                    last = pe.matmul(dst[:, c * 512:(c + 1) * 512], xs1[:, u, 0:P],
                                     w.rearrange("p a n -> p (a n)"), start=True, stop=True)
                last.then_inc(S[done], 1)

            def transpose_all(dst, src, done):
                for f in range(FT):
                    last = pe.transpose(dst[:, f * P:(f + 1) * P], src[:, f * P:(f + 1) * P], ident)
                last.then_inc(S[done], 1)

            def score(n, u, dst):
                pe.wait_ge(S["qT_copied"], n + 1)
                pe.wait_ge(S["kT_copied"], n + 1)
                for f in range(FT):
                    for w in range(NW):
                        rows = slice(WIN * w, WIN * (w + 1))
                        last = pe.matmul(dst[rows, f * P:(f + 1) * P], qT[:, f, rows],
                                         kT[:, u, f, :, WIN * w:WIN * (w + 2)], start=True, stop=True)
                last.then_inc(S["scores_done"], 1)

            def attend(n, dst):
                pe.wait_ge(S["pT_copied"], n + 1)
                pe.wait_ge(S["v_spread"], 16 * 4 * NW * (n + 1))
                for f in range(FT):
                    for w in range(NW):
                        rows = slice(WIN * w, WIN * (w + 1))
                        last = pe.matmul(dst[rows, f * P:(f + 1) * P], pT[:, f, rows], vwin[:, w, :, f, :],
                                         start=True, stop=True)
                last.then_inc(S["vwin_free"], 1)

            def out_project(n):
                pe.wait_ge(S["attnT_copied"], n + 1)
                pe.wait_ge(S["wo_loaded"], 16 * (n // NB + 1))
                for f in range(FT):
                    last = pe.matmul(pm[:, 512:512 + P], wo[:, f, :], attnT[:, f, :], start=(f == 0),
                                     stop=(f == FT - 1))
                last.then_inc(S["wo_done"], 1)

            def ff_mean(n):
                pe.wait_ge(S["shifted2"], n + 1)
                if not (isinstance(n, int) and n == 0):
                    pe.wait_ge(S["x_ready"], NB + n)
                pe.matmul(pm[:, 0:P], mean_w, xs2[:, 0:P], start=True, stop=True).then_inc(S["mean_done"], 1)

            def ff_var(n):
                pe.wait_ge(S["xc_squared"], n + 1)
                pe.matmul(pm[:, 0:P], mean_w, xcsq[:, :], start=True, stop=True)\
                  .then_inc(S["var_done"], 1)

            def ff_up(n):
                pe.wait_ge(S["xn2_ready"], n + 1)
                if runs(n + 1):
                    pe.wait_ge(S["residual1"], n + 2)
                pe.wait_ge(S["w1_loaded"], 16 * (n // NB + 1))
                for half in range(2):
                    for t, (at, rows) in enumerate(FFT):
                        last = pe.matmul(pm[0:rows, 512 * half + t * P:512 * half + (t + 1) * P],
                                         w1[:, half * FF + at:half * FF + at + rows], xn2[:, :],
                                         start=True, stop=True)
                last.then_inc(S["up_done"], 1)

            def ff_down(n):
                pe.wait_ge(S["gated"], 3 * (n + 1))
                pe.wait_ge(S["w2_loaded"], 48 * (n // NB + 1))
                for t, (at, rows) in enumerate(FFT):
                    last = pe.matmul(pm[:, 0:P], w2[0:rows, t, :], hid[0:rows, t, :], start=(t == 0),
                                     stop=(t == 2))
                last.then_inc(S["down_done"], 1)

            def step(n, u):
                a, b, c = slots(u)
                if runs(n):
                    if isinstance(n, int) and n == 0:
                        pe.wait_ge(S["k_turned"], 3 * 2)
                    score(n, u, c)
                if runs(n - 2):
                    ff_up(n - 2)
                if runs(n + 2):
                    if isinstance(n, int) and n == -1:
                        pe.wait_ge(S["q_turned"], 3)
                    project(n + 2, u, 0, a, "q_proj")
                    project(n + 2, u, 1, b, "k_proj")
                if runs(n + 1):
                    if runs(n):
                        pe.wait_ge(S["masked"], n + 1)
                    else:
                        pe.wait_ge(S["k_turned"], 3)
                    project(n + 1, 1 - u, 2, c, "v_proj")
                if runs(n):
                    pe.wait_ge(S["exped"], n + 1)
                    if runs(n + 2):
                        pe.wait_ge(S["q_turned"], 3 * (n + 3))
                    transpose_all(a, probs[:, :, :].rearrange("p h k -> p (h k)"), "pT_done")
                if runs(n + 1):
                    pe.wait_ge(S["q_scaled"], n + 2)
                    pe.wait_ge(S["v_copied"], n + 2)
                    transpose_all(c, rot[:, 1 - u, 0, :, :, :].rearrange("p h a d -> p (h a d)"), "qT_done")
                if runs(n):
                    if runs(n + 2):
                        pe.wait_ge(S["k_turned"], 3 * (n + 3))
                    attend(n, b)
                if runs(n - 2):
                    ff_down(n - 2)
                if runs(n + 1):
                    if not runs(n):
                        pe.wait_ge(S["q_turned"], 3 * 2)
                    pe.wait_ge(S["k_scaled"], n + 2)
                    transpose_all(a, rot[:, 1 - u, 1, :, :, :].rearrange("p h a d -> p (h a d)"), "kT_done")
                if runs(n - 1):
                    ff_mean(n - 1)
                if runs(n):
                    pe.wait_ge(S["normed"], n + 1)
                    if runs(n + 1):
                        pe.wait_ge(S["qT_copied"], n + 2)
                    transpose_all(c, attn[:, :, :].rearrange("p h d -> p (h d)"), "attnT_done")
                if runs(n - 1):
                    ff_var(n - 1)
                if runs(n):
                    out_project(n)

            run(pe, step)

        @block.scalar
        def _(act):
            def stage(n, u):
                act.wait_ge(S["x_ready"], n + 1)
                if not (isinstance(n, int) and n == 0):
                    act.wait_ge(S["carried1"], n)
                x = slot(n)
                act.activation(xs1[0:64, u, 0:P], x[0:64, :], ACT.Copy)
                act.activation(xs1[64:P, u, 1:P + 1], x[64:P, :], ACT.Copy)
                act.activation(xs1[64:P, u, 0:1], carry1[64:P, bass.ds(n % BPB, 1)], ACT.Copy)\
                   .then_inc(S["staged1"], 1)
                act.activation(carry1[64:P, bass.ds(n % BPB + 1, 1)],
                               xT[64:P, bass.ds((n % NB) * P + P - 1, 1)], ACT.Copy).then_inc(S["carried1"], 1)

            def copy_k(n, u, src):
                act.wait_ge(S["kT_done"], n + 1)
                src = src[:, :].rearrange("p (f t) -> p f t", f=FT)
                for s in range(2):
                    rows = slice(64 * s, 64 * s + 64)
                    act.activation(kT[rows, 1 - u, :, s, 0:WIN], src[rows, :, P - WIN:P], ACT.Copy)
                    last = act.activation(kT[rows, u, :, s, WIN:WIN + P], src[rows, :, :], ACT.Copy)
                last.then_inc(S["kT_copied"], 1)

            def square(n, k, src, proj, done):
                act.wait_ge(S[proj], n + 1)
                act.activation(squares[:, k, :], src[:, :], ACT.Square).then_inc(S[done], 1)

            def copy_v(n, u, src):
                act.wait_ge(S["v_proj"], n + 1)
                if not (isinstance(n, int) and n == 0):
                    act.wait_ge(S["v_spread"], 16 * 4 * NW * n)
                act.activation(vtok[:, u, :, :, :].rearrange("p s f d -> p f s d"),
                               src[:, :].rearrange("p (f s d) -> p f s d", f=FT, s=2), ACT.Copy)\
                   .then_inc(S["v_copied"], 1)

            def root_qk(n):
                act.wait_ge(S["q_summed"], n + 1)
                act.wait_ge(S["k_summed"], n + 1)
                act.activation(norms[:, :, :], ss[:, :, :], ACT.Sqrt).then_inc(S["qk_rooted"], 1)

            def root_var(n):
                act.wait_ge(S["var_done"], n + 1)
                act.activation(std[:, :], pm[:, 0:P], ACT.Sqrt, bias=eps[:, 0:1]).then_inc(S["std_rooted"], 1)

            def exp(n):
                act.wait_ge(S["max_taken"], n + 1)
                act.activation(probs[:, :, :], sm[:, :, :], ACT.Exp, scale=SCORE_SCALE)\
                   .then_inc(S["exped"], 1)

            def copy_out(src, dst, waits, done, n):
                act.wait_ge(S[waits], n + 1)
                act.activation(dst[:, :, :].rearrange("p f t -> p (f t)"), src[:, :], ACT.Copy)\
                   .then_inc(S[done], 1)

            def ff_square(n):
                act.wait_ge(S["centered"], n + 1)
                act.activation(xcsq[:, :], xc[:, :], ACT.Square).then_inc(S["xc_squared"], 1)

            def ff_gelu(n):
                act.wait_ge(S["up_done"], n + 1)
                for t, (at, rows) in enumerate(FFT):
                    last = act.activation(gate[0:rows, t, :], pm[0:rows, 512 + t * P:512 + (t + 1) * P],
                                          ACT.Gelu, bias=b1[0:rows, t, bass.ds(2 * (n // NB) + 1, 1)])
                last.then_inc(S["gelued"], 1)

            def step(n, u):
                a, b, c = slots(u)
                if runs(n + 1):
                    root_qk(n + 1)
                if runs(n - 2):
                    root_var(n - 2)
                if runs(n + 2):
                    square(n + 2, 0, a, "q_proj", "q_squared")
                    square(n + 2, 1, b, "k_proj", "k_squared")
                if runs(n):
                    exp(n)
                if runs(n + 1):
                    copy_v(n + 1, 1 - u, c)
                if runs(n):
                    copy_out(a, pT, "pT_done", "pT_copied", n)
                if runs(n + 1):
                    copy_out(c, qT, "qT_done", "qT_copied", n + 1)
                if runs(n - 2):
                    ff_gelu(n - 2)
                if runs(n + 1):
                    copy_k(n + 1, 1 - u, a)
                if runs(n + 3):
                    stage(n + 3, 1 - u)
                if runs(n - 1):
                    ff_square(n - 1)
                if runs(n):
                    copy_out(c, attnT, "attnT_done", "attnT_copied", n)

            act.wait_ge(S["tables_loaded"], 7 * 16)
            act.wait_ge(S["cleared_pool"], 3)
            act.wait_ge(S["cleared"], 1)
            stage(0, 0)
            run(act, step)

        @block.vector
        def _(dve):
            def tables(entry, layer, parity):
                dve.tensor_tensor(table[:, bass.ds(parity * BPB + entry, 1), :, :]
                                  .rearrange("p a k d -> p (a k d)"),
                                  rope[:, bass.ds(entry, 1), :, :].rearrange("p a k d -> p (a k d)"),
                                  scales[:, bass.ds(layer, 1), :, :].rearrange("p a k d -> p (a k d)"),
                                  ALU.mult).then_inc(S["tabled"], 1)

            def turn(n, u, k, src, squared, turned, added):
                dve.wait_ge(S[squared], n + 1)
                if not (isinstance(n, int) and n == 0):
                    dve.wait_ge(S[added], n)
                entry = ((n // NB) % 2) * BPB + n % BPB
                cos = table[:, bass.ds(entry, 1), 2 * k, :].rearrange("p a d -> p (a d)")
                v = src[:, :].rearrange("p (h a d) -> p h a d", h=HEADS, a=2)
                dve.tensor_tensor(rot[:, u, k, :, :, :].rearrange("p h a d -> p h (a d)"),
                                  src[:, :].rearrange("p (h d) -> p h d", h=HEADS),
                                  bcast(cos, 1, HEADS), ALU.mult).then_inc(S[turned], 1)
                for a in range(2):
                    sin = table[:, bass.ds(entry, 1), 2 * k + 1, 32 * a:32 * a + 32]\
                        .rearrange("p a d -> p (a d)")
                    dve.tensor_tensor(rot_sin[:, k, :, a, :], v[:, :, 1 - a, :], bcast(sin, 1, HEADS),
                                      ALU.mult).then_inc(S[turned], 1)

            def norm_square(k, summed):
                dve.tensor_reduce(ss[:, k, :], squares[:, k, :].rearrange("p (h d) -> p h d", h=HEADS),
                                  AX.X, ALU.add).then_inc(S[summed], 1)

            def invert_norms(n):
                dve.wait_ge(S["qk_rooted"], n + 1)
                dve.tensor_scalar(norms[:, :, :], norms[:, :, :], 1e-12, None, ALU.max)\
                   .then_inc(S["floored"], 1)
                dve.wait_ge(S["floored"], n + 1)
                dve.reciprocal(rnorm[:, :, :], norms[:, :, :]).then_inc(S["rnorm_ready"], 1)

            def mask(n, u, src):
                dve.wait_ge(S["scores_done"], n + 1)
                m = window[:, bass.ds((n // 2) % 4, 1), :].rearrange("p a k -> p (a k)") if u == 0 \
                    else window[:, 1, :]
                dve.tensor_tensor(sm[:, :, :], src[:, :].rearrange("p (h k) -> p h k", h=HEADS),
                                  bcast(m, 1, HEADS), ALU.add).then_inc(S["masked"], 1)
                dve.wait_ge(S["masked"], n + 1)
                dve.tensor_reduce(rowmax[:, :], sm[:, :, :], AX.X, ALU.max).then_inc(S["maxed"], 1)

            def sums(n):
                dve.wait_ge(S["exped"], n + 1)
                dve.tensor_reduce(rowsum[:, :], probs[:, :, :], AX.X, ALU.add).then_inc(S["summed"], 1)
                dve.wait_ge(S["summed"], n + 1)
                dve.reciprocal(rinv[:, :], rowsum[:, :]).then_inc(S["inverted"], 1)

            def normalise(n, src):
                dve.wait_ge(S["vwin_free"], n + 2)
                dve.wait_ge(S["inverted"], n + 1)
                dve.tensor_tensor(attn[:, :, :], src[:, :].rearrange("p (h d) -> p h d", h=HEADS),
                                  bcast(rinv[:, :], 2, DH), ALU.mult).then_inc(S["normed"], 1)

            def residual1(n, u):
                dve.wait_ge(S["wo_done"], n + 1)
                y, x = pm[:, 512:512 + P], slot(n)
                dve.tensor_tensor(xs2[0:64, 0:P], y[0:64, :], x[0:64, :], ALU.add)
                dve.tensor_tensor(xs2[64:P, 1:P + 1], y[64:P, :], x[64:P, :], ALU.add)
                if not (isinstance(n, int) and n == 0):
                    dve.wait_ge(S["carried2"], n)
                dve.tensor_copy(xs2[64:P, 0:1], carry2[64:P, bass.ds(n % BPB, 1)]).then_inc(S["shifted2"], 1)
                dve.tensor_tensor(xp[:, u, :], y, x, ALU.add).then_inc(S["residual1"], 1)
                dve.wait_ge(S["residual1"], n + 1)
                dve.tensor_copy(carry2[64:P, bass.ds(n % BPB + 1, 1)], xp[64:P, u, P - 1:P])\
                   .then_inc(S["carried2"], 1)

            def center(n):
                dve.wait_ge(S["mean_done"], n + 1)
                dve.tensor_tensor(xc[:, :], xs2[:, 0:P], pm[:, 0:P], ALU.subtract).then_inc(S["centered"], 1)

            def ff_norm(n):
                dve.wait_ge(S["std_rooted"], n + 1)
                dve.reciprocal(rstd[:, :], std[:, :]).then_inc(S["rstd_ready"], 1)
                dve.wait_ge(S["rstd_ready"], n + 1)
                dve.tensor_tensor(xhat[:, :], xc[:, :], rstd[:, :], ALU.mult).then_inc(S["hatted"], 1)
                dve.wait_ge(S["hatted"], n + 1)
                layer = n // NB
                dve.tensor_scalar(xn2[:, :], xhat[:, :], cols[:, 0, bass.ds(layer, 1)],
                                  cols[:, 1, bass.ds(layer, 1)], ALU.mult, ALU.add)\
                   .then_inc(S["xn2_ready"], 1)

            def ff_gate(n):
                dve.wait_ge(S["gelued"], n + 1)
                for t, (at, rows) in enumerate(FFT):
                    dve.scalar_tensor_tensor(out=hid[0:rows, t, :], in0=pm[0:rows, t * P:(t + 1) * P],
                                             scalar=b1[0:rows, t, bass.ds(2 * (n // NB), 1)],
                                             in1=gate[0:rows, t, :], op0=ALU.add, op1=ALU.mult)\
                       .then_inc(S["gated"], 1)

            def residual2(n, u):
                dve.wait_ge(S["down_done"], n + 1)
                dve.scalar_tensor_tensor(out=slot(n), in0=pm[:, 0:P], scalar=cols[:, 2, bass.ds(n // NB, 1)],
                                         in1=xp[:, u, :], op0=ALU.add, op1=ALU.add).then_inc(S["x_ready"], 1)

            def step(n, u):
                a, b, c = slots(u)
                if runs(n + 1):
                    invert_norms(n + 1)
                if runs(n - 1):
                    residual1(n - 1, 1 - u)
                if runs(n - 2):
                    ff_norm(n - 2)
                if runs(n):
                    mask(n, u, c)
                if u == 0 and runs(n) and not (isinstance(n, int) and n >= STEPS - 2):
                    tables((n // 2) % BPB, (n // NB + 1) % LAYERS, (n // NB + 1) % 2)
                if runs(n + 2):
                    if u == 0:
                        dve.wait_ge(S["tabled"], BPB + n // 2 + 1)
                    turn(n + 2, u, 0, a, "q_squared", "q_turned", "q_added")
                    turn(n + 2, u, 1, b, "k_squared", "k_turned", "k_added")
                if runs(n):
                    sums(n)
                if runs(n - 2):
                    ff_gate(n - 2)
                if runs(n + 2):
                    norm_square(0, "q_summed")
                if runs(n):
                    normalise(n, b)
                if runs(n - 2):
                    residual2(n - 2, u)
                if runs(n + 2):
                    norm_square(1, "k_summed")
                if runs(n - 1):
                    center(n - 1)

            dve.memset(carry1[:, :], 0.0).then_inc(S["cleared"], 1)
            dve.memset(carry2[:, :], 0.0).then_inc(S["x_ready"], NB)
            dve.wait_ge(S["tables_loaded"], 7 * 16)
            for entry in range(BPB):
                tables(entry, 0, 0)
            dve.wait_ge(S["tabled"], BPB)
            run(dve, step)

        @block.gpsimd
        def _(pool):
            pool.memset(kT[:, :, :, :, :], 0.0).then_inc(S["cleared_pool"], 1)
            pool.memset(vwin[:, :, :, :, :], 0.0).then_inc(S["vwin_free"], 1)
            pool.memset(vtok[:, :, :, :, :], 0.0).then_inc(S["cleared_pool"], 1)
            pool.memset(xs1[:, :, :], 0.0).then_inc(S["cleared_pool"], 1)

            def add(n, u, k, turned, added):
                pool.wait_ge(S[turned], 3 * (n + 1))
                r = rot[:, u, k, :, :, :].rearrange("p h a d -> p h (a d)")
                pool.tensor_tensor(r, r, rot_sin[:, k, :, :, :].rearrange("p h a d -> p h (a d)"), ALU.add)\
                    .then_inc(S[added], 1)

            def scale(n, u, k, added, scaled):
                pool.wait_ge(S[added], n + 1)
                pool.wait_ge(S["rnorm_ready"], n + 1)
                r = rot[:, u, k, :, :, :].rearrange("p h a d -> p h (a d)")
                pool.tensor_tensor(r, r, bcast(rnorm[:, k, :], 2, DH), ALU.mult).then_inc(S[scaled], 1)

            def take_max(n):
                pool.wait_ge(S["maxed"], n + 1)
                pool.tensor_tensor(sm[:, :, :], sm[:, :, :], bcast(rowmax[:, :], 2, 2 * WIN), ALU.subtract)\
                    .then_inc(S["max_taken"], 1)

            def step(n, u):
                if runs(n + 1):
                    scale(n + 1, 1 - u, 0, "q_added", "q_scaled")
                if runs(n):
                    take_max(n)
                if runs(n + 1):
                    scale(n + 1, 1 - u, 1, "k_added", "k_scaled")
                if runs(n + 2):
                    add(n + 2, u, 0, "q_turned", "q_added")
                    add(n + 2, u, 1, "k_turned", "k_added")

            run(pool, step)


def last_norm(nc, outer, x1, xT, ident, eps, out):
    with ExitStack() as ctx:
        y = ctx.enter_context(nc.sbuf_tensor("y", [P, NB, P], F32))
        ps = ctx.enter_context(nc.psum_tensor("ps_last", [P, NB * P], F32))
        turned = ctx.enter_context(nc.semaphore("turned"))
        added = ctx.enter_context(nc.semaphore("added"))
        stored = ctx.enter_context(nc.semaphore("stored"))
        norm = Norm(nc, ctx, "ln_last", eps[:, 0:1])
        block = ctx.enter_context(nc.Block())

        @block.tensor
        def _(pe):
            for n in range(NB):
                last = pe.transpose(ps[:, n * P:(n + 1) * P], xT[:, n * P:(n + 1) * P], ident)
            last.then_inc(turned, 1)

        @block.scalar
        def _(act):
            norm.scalar(act, 1, y[:, :, :])

        @block.vector
        def _(dve):
            dve.wait_ge(turned, 1)
            norm.vector(dve, 1, ps[:, :].rearrange("p (n d) -> p n d", n=NB), y[:, :, :])
            dve.wait_ge(norm.done, 1)
            dve.tensor_tensor(y[:, :, :], y[:, :, :], x1[:, :, :], ALU.add).then_inc(added, 1)

        @block.sync
        def _(sp):
            sp.wait_ge(added, 1)
            sp.dma_start(out.rearrange("(n p) d -> p n d", p=P), y[:, :, :]).then_inc(stored, 16)
            sp.wait_ge(stored, 16)


def _constants(np):
    eye = np.eye(P)
    i = np.arange(P)
    causal = (i[:, None] <= i[None, :]).astype(float)
    blocks = (i[:, None] // LD == i[None, :] // LD).astype(float)
    square = np.stack([eye, np.full((P, P), 1.0 / P), causal, blocks], 1).astype(np.float32)
    head = (i[:, None] // LD == np.arange(LH)[None, :]).astype(np.float32)
    q = (i % WIN)[:, None]
    k = np.arange(2 * WIN)[None, :]
    allowed = (q <= k) & (k <= q + WIN)
    first = allowed & ((i[:, None] >= WIN) | (k >= WIN))
    window = np.where(np.stack([first, allowed, allowed, allowed], 1), 0.0, MASKED).astype(np.float32)
    half = np.arange(0, DH, 2, dtype=np.float32)
    inv_freq = np.float32(1.0) / np.float32(10000.0) ** (half / np.float32(DH))
    t = np.arange(SEQ, dtype=np.float32)
    freqs = t[:, None] * inv_freq[None, :]
    base = (half + np.float32(0.4 * DH)) / np.float32(1.4 * DH)
    power = (t - SEQ // 2) / np.float32(WIN // 2)
    scale = base[None, :] ** power[:, None]
    cos, sin = np.cos(freqs), np.sin(freqs)
    both = lambda a, b: np.concatenate([a, b], -1)
    parts = [both(cos * scale, cos * scale), both(-sin * scale, sin * scale),
             both(cos / scale, cos / scale), both(-sin / scale, sin / scale)]
    rope = np.stack(parts, 1).reshape(BPB, P, 4, DH).transpose(1, 0, 2, 3).astype(np.float32)
    return square, head, window, np.ascontiguousarray(rope)


def kernel(L0_attn_X, L0_attn_Wq, L0_attn_Wv, L0_attn_q_norm_w, L0_attn_v_norm_w, L0_ffn_Wqkv,
           L0_ffn_q_scale, L0_ffn_k_scale, L0_ffn_Wo, L0_ffn_ln_g, L0_ffn_ln_b, L0_ffn_W1, L0_ffn_b1,
           L0_ffn_W2, L0_ffn_b2):
    import numpy as np
    import concourse.bacc as bacc
    from concourse.bass_utils import run_bass_kernel_spmd

    a = np.asarray
    square, head, window, rope = _constants(np)
    qs, ks = a(L0_ffn_q_scale), a(L0_ffn_k_scale)
    laid = {
        "x": a(L0_attn_X).reshape(BATCH * SEQ, P),
        "wqv": np.concatenate([a(L0_attn_Wq).T, a(L0_attn_Wv).T], 1),
        "lin_w": np.concatenate([a(L0_attn_q_norm_w).reshape(-1), a(L0_attn_v_norm_w).reshape(-1)]),
        "wqkv": a(L0_ffn_Wqkv),
        "scales": np.stack([qs, np.roll(qs, DH // 2, 1), ks, np.roll(ks, DH // 2, 1)], 1),
        "wo": a(L0_ffn_Wo),
        "w1": a(L0_ffn_W1),
        "b1": a(L0_ffn_b1).reshape(LAYERS, 2, FF).transpose(2, 0, 1).reshape(FF, 2 * LAYERS),
        "w2": a(L0_ffn_W2),
        "cols": np.stack([a(L0_ffn_ln_g).T, a(L0_ffn_ln_b).T, a(L0_ffn_b2).T], 1),
        "square": square, "head": head, "window": window, "rope": rope,
    }
    laid = {f"in_{name}": np.ascontiguousarray(v) for name, v in laid.items()}
    nc = bacc.Bacc("TRN2", target_bir_lowering=False, num_devices=1)
    args = [nc.dram_tensor(name, v.shape, mybir.dt.from_np(v.dtype), kind="ExternalInput").ap()
            for name, v in laid.items()]
    out = nc.dram_tensor("out_x", (BATCH * SEQ, P), F32, kind="ExternalOutput").ap()
    build(nc, *args, out)
    r = run_bass_kernel_spmd(nc, [laid], core_ids=[0])
    return r.results[0]["out_x"].reshape(BATCH, SEQ, P)
```

```python
from contextlib import ExitStack

import concourse.bass as bass
from concourse import mybir

ALU = mybir.AluOpType
ACT = mybir.ActivationFunctionType
AX = mybir.AxisListType
F32 = mybir.dt.float32
I32 = mybir.dt.int32

P = 128
LAYERS = 6
BATCH, SEQ = 2, 1024
BPB = SEQ // P
NB = BATCH * BPB
PARTS = 4
PB = NB // PARTS
STEPS = LAYERS * NB
HEADS, DH = 16, 64
INNER = HEADS * DH
FT = INNER // P
WIN = 32
NW = P // WIN
FF = 341
FFT = [(0, 128), (128, 128), (256, FF - 256)]
LH, LD = 16, 8
LG = 4
LGH = LH // LG
SPREADS = 16 * 2 * (NW + 1)
MASKED = -4e37
SCORE_SCALE = 8.0
ROOTS = 2 * HEADS + 1
NEWTON = 3
ROOT_OPS = 3 + 3 * NEWTON
GUESS = float(0x5f3759df - 2 ** 22 - 2 ** 30)


def bcast(ap, axis, count):
    wide = ap.unsqueeze(axis)
    shape = list(wide.shape)
    shape[axis] = count
    return wide.broadcast_to(shape)


def build(nc, x_in, wqv_in, lin_w_in, wqkv_in, scales_in, wo_in, w1_in, b1_in, w2_in, cols_in,
          square_in, head_in, head_cols_in, window_in, rope_in, out):
    with ExitStack() as ctx:
        def sb(name, shape, stack=ctx):
            return stack.enter_context(nc.sbuf_tensor(name, shape, F32))

        def sem(name, stack=ctx):
            return stack.enter_context(nc.semaphore(name))

        x1 = sb("x1", [P, NB, P])
        xT = sb("xT", [P, NB * P])
        square = sb("square", [P, 4, P])
        eps = sb("eps", [P, 2])
        ident, mean_w, causal, head_blocks = (square[:, k, :] for k in range(4))
        weights = Weights(nc, ctx, wqkv_in, scales_in, wo_in, w1_in, b1_in, w2_in, cols_in, window_in, rope_in)
        linear_attention(nc, x_in, wqv_in, lin_w_in, square_in, head_in, head_cols_in, weights,
                         x1, xT, square, eps)
        layers(nc, weights, xT, ident, mean_w, eps)
        last_norm(nc, x1, xT, ident, eps, out)


class Weights:

    def __init__(self, nc, ctx, wqkv_in, scales_in, wo_in, w1_in, b1_in, w2_in, cols_in, window_in, rope_in):
        def sb(name, shape):
            return ctx.enter_context(nc.sbuf_tensor(name, shape, F32))

        def sem(name):
            return ctx.enter_context(nc.semaphore(name))

        self.wqkv = sb("wqkv", [P, 2, 3 * INNER])
        self.wo = sb("wo", [P, FT, P])
        self.w1 = sb("w1", [P, 2 * FF])
        self.w2 = sb("w2", [P, 3, P])
        self.b1 = sb("b1", [P, 3, 2 * LAYERS])
        self.cols = sb("cols", [P, 3, LAYERS])
        self.window = sb("window", [P, 4, WIN * 2])
        self.rope = sb("rope", [P, BPB, 4, DH])
        self.scales = sb("scales", [P, LAYERS, 4, DH])
        self.tables_loaded, self.wqkv_loaded, self.wo_loaded, self.w1_loaded, self.w2_loaded = (
            sem("tables_loaded"), sem("wqkv_loaded"), sem("wo_loaded"), sem("w1_loaded"), sem("w2_loaded"))
        self.wqkv_in, self.wo_in, self.w1_in, self.w2_in = wqkv_in, wo_in, w1_in, w2_in
        self.b1_in, self.cols_in, self.window_in, self.rope_in, self.scales_in = (
            b1_in, cols_in, window_in, rope_in, scales_in)

    def load_tables(self, sp):
        sp.dma_start(self.window[:, :, :], self.window_in).then_inc(self.tables_loaded, 16)
        sp.dma_start(self.rope[:, :, :, :], self.rope_in).then_inc(self.tables_loaded, 16)
        sp.dma_start(self.scales[:, :, :, :], self.scales_in.partition_broadcast(P)).then_inc(self.tables_loaded, 16)
        sp.dma_start(self.cols[:, :, :], self.cols_in).then_inc(self.tables_loaded, 16)
        for t, (at, rows) in enumerate(FFT):
            sp.dma_start(self.b1[0:rows, t, :], self.b1_in[at:at + rows, :]).then_inc(self.tables_loaded, 16)

    def load_wqkv(self, sp, layer):
        sp.dma_start(self.wqkv[:, bass.ds(layer % 2, 1), :], self.wqkv_in[bass.ds(layer, 1), :, :]
                     .rearrange("a p n -> p a n")).then_inc(self.wqkv_loaded, 16)

    def load_wo(self, sp, layer):
        sp.dma_start(self.wo[:, :, :], self.wo_in[bass.ds(layer, 1), :, :]
                     .rearrange("a (f p) n -> p (a f) n", p=P)).then_inc(self.wo_loaded, 16)

    def load_w1(self, sp, layer):
        sp.dma_start(self.w1[:, :], self.w1_in[bass.ds(layer, 1), :, :].rearrange("a p n -> p (a n)"))\
          .then_inc(self.w1_loaded, 16)

    def load_w2(self, sp, layer):
        for t, (at, rows) in enumerate(FFT):
            sp.dma_start(self.w2[0:rows, t, :], self.w2_in[bass.ds(layer, 1), at:at + rows, :]
                         .rearrange("a p n -> p (a n)")).then_inc(self.w2_loaded, 16)


class Norm:

    def __init__(self, nc, ctx, tag, eps):
        self.eps = eps
        def sb(name, shape):
            return ctx.enter_context(nc.sbuf_tensor(f"{tag}_{name}", shape, F32))

        def sem(name):
            return ctx.enter_context(nc.semaphore(f"{tag}_{name}"))
        self.sq, self.mean, self.var = sb("sq", [P, NB, P]), sb("mean", [P, NB]), sb("var", [P, NB])
        self.std, self.rstd = sb("std", [P, NB]), sb("rstd", [P, NB])
        self.summed, self.meaned, self.centered = sem("summed"), sem("meaned"), sem("centered")
        self.squared, self.varsum, self.rooted = sem("squared"), sem("varsum"), sem("rooted")
        self.inverted, self.done = sem("inverted"), sem("done")

    def vector(self, dve, k, src, dst, ready):
        def center(q):
            at, mean = PARTS * k + q + 1, self.mean[:, q * PB:(q + 1) * PB]
            ready(q)
            dve.tensor_reduce(mean, src(q), AX.X, ALU.add).then_inc(self.summed, 1)
            dve.wait_ge(self.summed, at)
            dve.tensor_scalar(mean, mean, 1.0 / P, None, ALU.mult).then_inc(self.meaned, 1)
            dve.wait_ge(self.meaned, at)
            dve.tensor_tensor(dst(q), src(q), bcast(mean, 2, P), ALU.subtract).then_inc(self.centered, 1)

        def sum_squares(q):
            dve.wait_ge(self.squared, PARTS * k + q + 1)
            dve.tensor_reduce(self.var[:, q * PB:(q + 1) * PB], self.sq[:, q * PB:(q + 1) * PB, :], AX.X, ALU.add)\
               .then_inc(self.varsum, 1)

        def scale(q):
            at, rstd = PARTS * k + q + 1, self.rstd[:, q * PB:(q + 1) * PB]
            dve.wait_ge(self.rooted, at)
            dve.reciprocal(rstd, self.std[:, q * PB:(q + 1) * PB]).then_inc(self.inverted, 1)
            dve.wait_ge(self.inverted, at)
            dve.tensor_tensor(dst(q), dst(q), bcast(rstd, 2, P), ALU.mult).then_inc(self.done, 1)

        for i in range(PARTS + 2):
            if i < PARTS:
                center(i)
            if 0 <= i - 1 < PARTS:
                sum_squares(i - 1)
            if i >= 2:
                scale(i - 2)

    def scalar(self, act, k, dst, rooted=None):
        for i in range(PARTS + 1):
            if i < PARTS:
                act.wait_ge(self.centered, PARTS * k + i + 1)
                act.activation(self.sq[:, i * PB:(i + 1) * PB, :], dst(i), ACT.Square).then_inc(self.squared, 1)
            if i >= 1:
                part = slice((i - 1) * PB, i * PB)
                act.wait_ge(self.varsum, PARTS * k + i)
                act.activation(self.std[:, part], self.var[:, part], ACT.Sqrt, scale=1.0 / P, bias=self.eps)\
                   .then_inc(self.rooted, 1)
                if rooted:
                    rooted(i - 1)


def linear_attention(nc, x_in, wqv_in, lin_w_in, square_in, head_in, head_cols_in, weights,
                     x1, xT, square, eps):
    ident, _, causal, head_blocks = (square[:, k, :] for k in range(4))
    NH2 = 2 * LH
    with ExitStack() as ctx:
        def sb(name, shape):
            return ctx.enter_context(nc.sbuf_tensor(name, shape, F32))

        def sem(name):
            return ctx.enter_context(nc.semaphore(name))

        x = sb("x", [P, NB, P])
        wqv = sb("wqv", [P, 2 * P])
        lin_w = sb("lin_w", [P, 2 * P])
        head_of = sb("head_of", [P, LH])
        head_cols = sb("head_cols", [P, LGH, P // LG])
        xn = sb("xn", [P, NB, P])
        xnT = sb("xnT", [P, NB * P])
        qv = sb("qv", [P, NB, 2 * P])
        qvsq = sb("qvsq", [P, 2, PB, 2 * P])
        qvss = sb("qvss", [P, 2, PB * NH2])
        qvstd = sb("qvstd", [P, 2, PB * NH2])
        qvr = sb("qvr", [P, 2, PB * NH2])
        qT = sb("qT_lin", [P, NB * P])
        o = sb("o", [P, NB, P])
        k_tok = sb("k_tok", [P, 2, P])
        v_tok = sb("v_tok", [P, 2, P])
        k_feat = sb("k_feat", [P, 2, P])
        q_feat = sb("q_feat", [P, 2, P])
        q_heads = sb("q_heads", [P, 2, LH, P])
        v_heads = sb("v_heads", [P, 2, LG, LGH, P // LG])
        scores = sb("scores_lin", [P, 2, LH, P])
        state = sb("state", [P, P])
        delta = sb("delta", [P, P])
        oT = sb("oT", [P, P])
        ps = ctx.enter_context(nc.psum_tensor("ps_lin", [P, 4096], F32))
        psa = ps[:, 0:2048]
        psb = ps[:, 2048:4096]
        ps_out, ps_state, ps_turn = ps[:, 2048:2048 + P], ps[:, 2560:2560 + P], ps[:, 3072:3072 + P]

        x_loaded = [sem(f"x{q}_loaded") for q in range(PARTS)]
        w_loaded, c_loaded = sem("w_loaded"), sem("c_loaded")
        keysT_done, keysT_copied = sem("keysT_done"), sem("keysT_copied")
        qv_done, qv_squared, qv_summed = sem("qv_done"), sem("qv_squared"), sem("qv_summed")
        qv_rooted, qv_inverted, qv_scaled, qv_weighted = (
            sem("qv_rooted"), sem("qv_inverted"), sem("qv_scaled"), sem("qv_weighted"))
        qsT_done, qsT_copied = sem("qsT_done"), sem("qsT_copied")
        q_staged, k_staged, v_staged = sem("q_staged"), sem("k_staged"), sem("v_staged")
        heads_cut, v_cut = sem("heads_cut"), sem("v_cut")
        scored, causal_cut = sem("scored"), sem("causal_cut")
        out_done, oT_copied, out_turned = sem("out_done"), sem("oT_copied"), sem("out_turned")
        out_copied, state_done = sem("out_copied"), sem("state_done")
        delta_cut, state_kept = sem("delta_cut"), sem("state_kept")
        x1_summed, xT_done, eps_set = sem("x1_summed"), sem("xT_done"), sem("eps_set")
        norm = Norm(nc, ctx, "ln", eps[:, 0:1])
        block = ctx.enter_context(nc.Block())

        def part(tile):
            return lambda q: tile[:, q * PB:(q + 1) * PB, :]

        def bank(q):
            return slice(q * PB * P, (q + 1) * PB * P)

        def qv_place(q):
            return psb[:, (q % 2) * PB * 2 * P:(q % 2 + 1) * PB * 2 * P]

        def has_block(n):
            return not isinstance(n, int) or 0 <= n < NB

        def run(eng, step):
            for n in range(2):
                step(n, n)
            with eng.Fori(1, NB // 2 - 1) as j:
                step(2 * j, 0)
                step(2 * j + 1, 1)
            for n in range(NB - 2, NB):
                step(n, n % 2)

        def cut_heads(eng, n, u):
            eng.wait_ge(q_staged, n + 1)
            eng.tensor_tensor(q_heads[:, u, :, :], bcast(q_feat[:, u, :], 1, LH), bcast(head_of[:, :], 2, P),
                              ALU.mult).then_inc(heads_cut, 1)

        @block.sync
        def _(sp):
            for q in range(PARTS):
                sp.dma_start(part(x)(q), x_in[q * PB * P:(q + 1) * PB * P, :].rearrange("(n p) d -> p n d", p=P))\
                  .then_inc(x_loaded[q], 16)
            sp.dma_start(square[:, :, :], square_in).then_inc(c_loaded, 16)
            sp.dma_start(head_of[:, :], head_in).then_inc(c_loaded, 16)
            sp.dma_start(head_cols[:, :, :], head_cols_in.rearrange("(h j) -> h j", h=LGH).partition_broadcast(P))\
              .then_inc(c_loaded, 16)
            sp.dma_start(wqv[:, :], wqv_in).then_inc(w_loaded, 16)
            sp.dma_start(lin_w[:, :], lin_w_in.partition_broadcast(P)).then_inc(w_loaded, 16)
            weights.load_tables(sp)
            weights.load_wqkv(sp, 0)
            weights.load_wo(sp, 0)
            weights.load_w1(sp, 0)
            weights.load_w2(sp, 0)

        @block.tensor
        def _(pe):
            pe.wait_ge(c_loaded, 48)

            def turn_keys(q):
                pe.wait_ge(norm.done, q + 1)
                for n in range(q * PB, (q + 1) * PB):
                    last = pe.transpose(psa[:, n * P:(n + 1) * P], xn[:, n, :], ident)
                last.then_inc(keysT_done, 1)

            def project(q):
                if q >= 2:
                    pe.wait_ge(qv_scaled, q - 1)
                pe.wait_ge(keysT_copied, q + 1)
                for n in range(PB):
                    last = pe.matmul(qv_place(q)[:, n * 2 * P:(n + 1) * 2 * P],
                                     xnT[:, (q * PB + n) * P:(q * PB + n + 1) * P], wqv[:, :],
                                     start=True, stop=True)
                last.then_inc(qv_done, 1)

            turn_keys(0)
            pe.wait_ge(w_loaded, 32)
            for q in range(1, PARTS):
                turn_keys(q)
                project(q - 1)
            project(PARTS - 1)
            for q in range(PARTS):
                pe.wait_ge(qv_weighted, q + 1)
                for n in range(q * PB, (q + 1) * PB):
                    last = pe.transpose(psa[:, n * P:(n + 1) * P], qv[:, n, 0:P], ident)
                last.then_inc(qsT_done, 1)
            pe.wait_ge(qsT_copied, PARTS)

            def score(n, u):
                pe.wait_ge(k_staged, n + 1)
                pe.wait_ge(heads_cut, n + 1)
                for g in range(LG):
                    if not (isinstance(n, int) and n == 0):
                        pe.wait_ge(causal_cut, LG * (n - 1) + g + 1)
                    pe.matmul(psa[:, g * 512:(g + 1) * 512], k_feat[:, u, :],
                              q_heads[:, u, LGH * g:LGH * (g + 1), :], start=True, stop=True).then_inc(scored, 1)

            def turn_back(n):
                pe.wait_ge(oT_copied, n + 1)
                if not (isinstance(n, int) and n == 0):
                    pe.wait_ge(out_copied, n)
                pe.transpose(ps_turn, oT[:, :], ident).then_inc(out_turned, 1)

            def outputs(n, u):
                pe.wait_ge(state_kept, n + 1)
                pe.wait_ge(v_cut, n + 1)
                pe.wait_ge(causal_cut, LG * (n + 1))
                if not (isinstance(n, int) and n == 0):
                    pe.wait_ge(oT_copied, n)
                pe.matmul(ps_out, state[:, :], qT[:, bass.ds(n * P, P)], start=True, stop=False,
                          skip_group_check=True)
                for h in range(LGH):
                    for g in range(LG):
                        rows = slice(g * (P // LG), (g + 1) * (P // LG))
                        last = pe.matmul(ps_out[rows, :], v_heads[:, u, g, h, :], scores[:, u, LGH * g + h, :],
                                         start=False, stop=(h == LGH - 1), skip_group_check=True)
                last.then_inc(out_done, 1)
                if not (isinstance(n, int) and n == 0):
                    pe.wait_ge(delta_cut, n)
                pe.matmul(ps_state, k_tok[:, u, :], v_tok[:, u, :], start=True, stop=True)\
                  .then_inc(state_done, 1)

            def step(n, u):
                if has_block(n + 1):
                    score(n + 1, 1 - u)
                if has_block(n - 1):
                    turn_back(n - 1)
                outputs(n, u)

            score(0, 0)
            run(pe, step)
            turn_back(NB - 1)
            for q in range(PARTS):
                pe.wait_ge(norm.done, 2 * PARTS + q + 1)
                for n in range(q * PB, (q + 1) * PB):
                    last = pe.transpose(psa[:, n * P:(n + 1) * P], o[:, n, :], ident)
                last.then_inc(xT_done, 1)

        @block.scalar
        def _(act):
            act.wait_ge(eps_set, 2)

            def stage_q(n, u):
                act.activation(q_feat[:, u, :], qT[:, bass.ds(n * P, P)], ACT.Copy).then_inc(q_staged, 1)

            def stage_k(n, u):
                act.activation(k_feat[:, u, :], xnT[:, bass.ds(n * P, P)], ACT.Copy).then_inc(k_staged, 1)

            def stage_v(n, u):
                act.activation(k_tok[:, u, :], xn[:, bass.ds(n, 1), :].rearrange("p a d -> p (a d)"), ACT.Copy)
                act.activation(v_tok[:, u, :], qv[:, bass.ds(n, 1), P:2 * P].rearrange("p a d -> p (a d)"),
                               ACT.Copy).then_inc(v_staged, 1)

            def copy_back(n):
                act.wait_ge(out_turned, n + 1)
                act.activation(o[:, bass.ds(n, 1), :].rearrange("p a d -> p (a d)"), ps_turn, ACT.Copy)\
                   .then_inc(out_copied, 1)

            def step(n, u):
                if has_block(n + 2):
                    act.wait_ge(heads_cut, n + 1)
                    stage_q(n + 2, u)
                    act.wait_ge(scored, LG * (n + 1))
                    stage_k(n + 2, u)
                if has_block(n - 1):
                    copy_back(n - 1)
                act.wait_ge(out_done, n + 1)
                act.activation(oT[:, :], ps_out, ACT.Copy).then_inc(oT_copied, 1)
                if has_block(n + 2):
                    act.wait_ge(state_done, n + 1)
                    stage_v(n + 2, u)

            def copy_keys(q):
                act.wait_ge(keysT_done, q + 1)
                act.activation(xnT[:, bank(q)], psa[:, bank(q)], ACT.Copy).then_inc(keysT_copied, 1)

            norm.scalar(act, 0, part(xn), rooted=lambda q: copy_keys(q - 1) if q else None)
            copy_keys(PARTS - 1)
            for i in range(PARTS + 1):
                if i < PARTS:
                    if i >= 2:
                        act.wait_ge(qv_summed, i - 1)
                    act.wait_ge(qv_done, i + 1)
                    act.activation(qvsq[:, i % 2, :, :], qv_place(i).rearrange("p (n d) -> p n d", n=PB),
                                   ACT.Square).then_inc(qv_squared, 1)
                if i >= 1:
                    u = (i - 1) % 2
                    act.wait_ge(qv_summed, i)
                    act.activation(qvstd[:, u, :], qvss[:, u, :], ACT.Sqrt, scale=1.0 / LD, bias=eps[:, 1:2])\
                       .then_inc(qv_rooted, 1)
            for q in range(PARTS):
                act.wait_ge(qsT_done, q + 1)
                act.activation(qT[:, bank(q)], psa[:, bank(q)], ACT.Copy).then_inc(qsT_copied, 1)
                if q == 0:
                    act.wait_ge(qsT_copied, 1)
                    act.wait_ge(qv_weighted, 1)
                    for n in range(2):
                        stage_q(n, n)
                        stage_k(n, n)
                        stage_v(n, n)
            act.wait_ge(qsT_copied, PARTS)
            act.wait_ge(qv_weighted, PARTS)
            run(act, step)
            copy_back(NB - 1)

            def copy_x(q):
                act.wait_ge(xT_done, q + 1)
                act.activation(xT[:, bank(q)], psa[:, bank(q)], ACT.Copy)

            norm.scalar(act, 1, part(o))
            norm.scalar(act, 2, part(o), rooted=lambda q: copy_x(q - 1) if q else None)
            copy_x(PARTS - 1)

        @block.vector
        def _(dve):
            norm.vector(dve, 0, part(x), part(xn), lambda q: dve.wait_ge(x_loaded[q], 16))
            for i in range(PARTS + 1):
                if i < PARTS:
                    dve.wait_ge(qv_squared, i + 1)
                    dve.tensor_reduce(qvss[:, i % 2, :], qvsq[:, i % 2, :, :].rearrange("p n (h d) -> p (n h) d", d=LD),
                                      AX.X, ALU.add).then_inc(qv_summed, 1)
                if i >= 1:
                    q, u = i - 1, (i - 1) % 2
                    dve.wait_ge(qv_rooted, i)
                    dve.reciprocal(qvr[:, u, :], qvstd[:, u, :]).then_inc(qv_inverted, 1)
                    dve.wait_ge(qv_inverted, i)
                    dve.tensor_tensor(part(qv)(q).rearrange("p n (h d) -> p (n h) d", d=LD),
                                      qv_place(q).rearrange("p (m d) -> p m d", d=LD),
                                      bcast(qvr[:, u, :], 2, LD), ALU.mult).then_inc(qv_scaled, 1)
            dve.wait_ge(c_loaded, 48)

            def cut_scores(n, u):
                for g in range(LG):
                    dve.wait_ge(scored, LG * n + g + 1)
                    if not (isinstance(n, int) and n < 2):
                        dve.wait_ge(out_done, n - 1)
                    dve.tensor_tensor(scores[:, u, LGH * g:LGH * (g + 1), :],
                                      psa[:, g * 512:(g + 1) * 512].rearrange("p (h q) -> p h q", h=LGH),
                                      bcast(causal, 1, LGH), ALU.mult).then_inc(causal_cut, 1)

            cut_heads(dve, 0, 0)
            cut_scores(0, 0)
            for b in range(BATCH):
                base = b * BPB
                dve.memset(state[:, :], 0.0).then_inc(state_kept, 1)

                def step(n, u):
                    if has_block(n + 1):
                        cut_scores(n + 1, 1 - u)
                    dve.wait_ge(state_done, n + 1)
                    dve.tensor_tensor(delta[:, :], ps_state, head_blocks, ALU.mult).then_inc(delta_cut, 1)
                    if not (isinstance(n, int) and (n + 1) % BPB == 0):
                        dve.wait_ge(delta_cut, n + 1)
                        dve.wait_ge(state_kept, n + 1)
                        dve.tensor_tensor(state[:, :], state[:, :], delta[:, :], ALU.add)\
                           .then_inc(state_kept, 1)

                for n in range(2):
                    step(base + n, n)
                with dve.Fori(base // 2 + 1, (base + BPB) // 2 - 1) as j:
                    step(2 * j, 0)
                    step(2 * j + 1, 1)
                for n in range(base + BPB - 2, base + BPB):
                    step(n, n % 2)
            norm.vector(dve, 1, part(o), part(o), lambda q: dve.wait_ge(out_copied, PB * (q + 1)))
            norm.vector(dve, 2, part(x1), part(o), lambda q: dve.wait_ge(x1_summed, q + 1))

        @block.gpsimd
        def _(pool):
            pool.memset(eps[:, 0:1], 1e-5).then_inc(eps_set, 1)
            pool.memset(eps[:, 1:2], 1e-8).then_inc(eps_set, 1)
            pool.wait_ge(w_loaded, 32)
            for q in range(PARTS):
                pool.wait_ge(qv_scaled, q + 1)
                pool.tensor_tensor(part(qv)(q), part(qv)(q), bcast(lin_w[:, :], 1, PB), ALU.mult)\
                    .then_inc(qv_weighted, 1)

            def cut_values(n, u):
                pool.wait_ge(v_staged, n + 1)
                pool.tensor_tensor(v_heads[:, u, :, :, :],
                                   bcast(v_tok[:, u, :].rearrange("p (g j) -> p g j", g=LG), 2, LGH),
                                   bcast(head_cols[:, :, :], 1, LG), ALU.mult).then_inc(v_cut, 1)

            def step(n, u):
                if has_block(n + 2):
                    pool.wait_ge(scored, LG * (n + 1))
                    cut_heads(pool, n + 2, u)
                if has_block(n + 1):
                    if has_block(n - 1):
                        pool.wait_ge(out_done, n)
                    cut_values(n + 1, 1 - u)

            pool.wait_ge(c_loaded, 48)
            pool.wait_ge(heads_cut, 1)
            cut_heads(pool, 1, 1)
            cut_values(0, 0)
            run(pool, step)
            for q in range(PARTS):
                pool.wait_ge(norm.done, PARTS + q + 1)
                pool.tensor_tensor(part(x1)(q), part(x)(q), part(o)(q), ALU.add).then_inc(x1_summed, 1)


def layers(nc, weights, xT, ident, mean_w, eps):
    with ExitStack() as ctx:
        def sb(name, shape):
            return ctx.enter_context(nc.sbuf_tensor(name, shape, F32))

        def sem(name):
            return ctx.enter_context(nc.semaphore(name))

        def psum(name):
            return ctx.enter_context(nc.psum_tensor(name, [P, 1024], F32))

        wqkv, wo, w1, w2, b1, cols = weights.wqkv, weights.wo, weights.w1, weights.w2, weights.b1, weights.cols
        window, rope, scales = weights.window, weights.rope, weights.scales
        table = sb("table", [P, 2, 4, DH])
        xs1 = sb("xs1", [P, 2, P + 1])
        carry1 = sb("carry1", [P, BPB + 1])
        squares = sb("squares", [P, 2, INNER])
        ss = sb("ss", [P, 2, HEADS])
        minus_half = sb("minus_half", [P, ROOTS])
        root_t = sb("root_t", [P, ROOTS])
        root = sb("root", [P, ROOTS])
        warm = sb("warm", [P, 1])
        warm_exp = sb("warm_exp", [P, 1])
        rot = sb("rot", [P, 2, 2, HEADS, 2, DH // 2])
        rot_sin = sb("rot_sin", [P, 2, HEADS, 2, DH // 2])
        qT = sb("qT", [P, FT, P])
        kT = sb("kT", [P, 2, FT, 2, WIN + P])
        vtok = sb("vtok", [P, 2, 2, FT, DH])
        vwin = sb("vwin", [P, NW, 2, FT, DH])
        sm = sb("sm", [P, HEADS, 2 * WIN])
        rowmax = sb("rowmax", [P, HEADS])
        probs = sb("probs", [P, HEADS, 2 * WIN])
        rowsum = sb("rowsum", [P, HEADS])
        rinv = sb("rinv", [P, HEADS])
        pT = sb("pT", [P, FT, P])
        attn = sb("attn", [P, HEADS, DH])
        attnT = sb("attnT", [P, FT, P])
        xs2 = sb("xs2", [P, P + 1])
        carry2 = sb("carry2", [P, BPB + 1])
        xc = sb("xc", [P, P])
        xcsq = sb("xcsq", [P, P])
        xhat = sb("xhat", [P, P])
        xn2 = sb("xn2", [P, P])
        gate = sb("gate", [P, 3, P])
        hid = sb("hid", [P, 3, P])
        r0, r1, r2, pm = psum("r0"), psum("r1"), psum("r2"), psum("pm")

        names = (
            "v_spread "
            "q_proj k_proj v_proj qT_done kT_done scores_done pT_done vwin_free attnT_done wo_done "
            "mean_done var_done rstd_spread up_done down_done "
            "staged1 carried1 qT_copied kT_copied k_carried q_squared k_squared v_copied exped pT_copied attnT_copied "
            "xc_squared gelued warmed warmed_exp "
            "cleared tabled q_turned k_turned q_summed k_summed refined "
            "masked maxed summed inverted normed residual1 shifted2 carried2 centered hatted "
            "xn2_ready gated x_ready "
            "cleared_pool max_taken q_folded k_folded q_added q_scaled k_added k_scaled"
        ).split()
        S = {name: sem(name) for name in names}
        S.update(tables_loaded=weights.tables_loaded, wqkv_loaded=weights.wqkv_loaded,
                 wo_loaded=weights.wo_loaded, w1_loaded=weights.w1_loaded, w2_loaded=weights.w2_loaded)
        block = ctx.enter_context(nc.Block())

        AHEAD, BEHIND = 2, 3

        def runs(n):
            return not isinstance(n, int) or 0 <= n < STEPS

        def slots(u):
            return (r0, r1, r2) if u == 0 else (r0, r2, r1)

        def run(eng, step):
            for n in range(-AHEAD, 4):
                step(n, n % 2)
            with eng.Fori(2, STEPS // 2 - 1) as j:
                step(2 * j, 0)
                step(2 * j + 1, 1)
            for n in range(STEPS - 2, STEPS + BEHIND):
                step(n, n % 2)

        def slot(n):
            return xT[:, bass.ds((n % NB) * P, P)]

        @block.sync
        def _(sp):
            def spread_v(n, u):
                turn = n + 1 if isinstance(n, int) else sp.snap(n + 1)
                sp.wait_ge(S["v_copied"], turn)
                sp.wait_ge(S["vwin_free"], turn)
                for s in range(2):
                    at = 2 * WIN * s
                    sp.dma_start(vwin[at:at + WIN, 0, s, :, :], vtok[P - WIN:P, 1 - u, s, :, :])\
                      .then_inc(S["v_spread"], 16)
                    sp.dma_start(vwin[at + WIN:at + 2 * WIN, 0, s, :, :], vtok[0:WIN, u, s, :, :])\
                      .then_inc(S["v_spread"], 16)
                    for w in range(1, NW):
                        sp.dma_start(vwin[at:at + 2 * WIN, w, s, :, :],
                                     vtok[WIN * (w - 1):WIN * (w + 1), u, s, :, :]).then_inc(S["v_spread"], 16)

            sp.wait_ge(S["cleared_pool"], 1)
            for n in range(4):
                spread_v(n, n % 2)
            with sp.Fori(0, LAYERS - 1) as layer:
                sp.wait_ge(S["v_proj"], 2 * NB * layer + 2)
                weights.load_wqkv(sp, layer + 1)
                with sp.Fori(2, NB // 2) as j:
                    spread_v(layer * NB + 2 * j, 0)
                    spread_v(layer * NB + 2 * j + 1, 1)
                used = sp.snap(NB * (layer + 1))
                spread_v(used, 0)
                sp.wait_ge(S["wo_done"], used)
                weights.load_wo(sp, layer + 1)
                spread_v(used + 1, 1)
                spread_v(used + 2, 0)
                sp.wait_ge(S["up_done"], used)
                weights.load_w1(sp, layer + 1)
                spread_v(used + 3, 1)
                sp.wait_ge(S["down_done"], used)
                weights.load_w2(sp, layer + 1)
            with sp.Fori((STEPS - NB) // 2 + 2, STEPS // 2) as j:
                spread_v(2 * j, 0)
                spread_v(2 * j + 1, 1)

        @block.tensor
        def _(pe):
            def project(n, u, k, dst, done):
                pe.wait_ge(S["staged1"], n + 1)
                pe.wait_ge(S["wqkv_loaded"], 16 * (n // NB + 1))
                for c in range(2):
                    w = wqkv[:, bass.ds((n // NB) % 2, 1), k * INNER + c * 512:k * INNER + (c + 1) * 512]
                    pe.matmul(dst[:, c * 512:(c + 1) * 512], xs1[:, u, 0:P], w.rearrange("p a n -> p (a n)"),
                              start=True, stop=True).then_inc(S[done], 1)

            def transpose_all(dst, src, done):
                for f in range(FT):
                    last = pe.transpose(dst[:, f * P:(f + 1) * P], src[:, f * P:(f + 1) * P], ident)
                last.then_inc(S[done], 1)

            def score(n, u, dst):
                pe.wait_ge(S["qT_copied"], n + 1)
                pe.wait_ge(S["kT_copied"], n + 1)
                if not (isinstance(n, int) and n == 0):
                    pe.wait_ge(S["k_carried"], n)
                for f in range(FT):
                    for w in range(NW):
                        rows = slice(WIN * w, WIN * (w + 1))
                        last = pe.matmul(dst[rows, f * P:(f + 1) * P], qT[:, f, rows],
                                         kT[:, u, f, :, WIN * w:WIN * (w + 2)], start=True, stop=True)
                last.then_inc(S["scores_done"], 1)

            def attend(n, dst):
                pe.wait_ge(S["pT_copied"], n + 1)
                pe.wait_ge(S["v_spread"], SPREADS * (n + 1))
                for f in range(FT):
                    for w in range(NW):
                        rows = slice(WIN * w, WIN * (w + 1))
                        last = pe.matmul(dst[rows, f * P:(f + 1) * P], pT[:, f, rows], vwin[:, w, :, f, :],
                                         start=True, stop=True)
                last.then_inc(S["vwin_free"], 1)

            def out_project(n):
                pe.wait_ge(S["attnT_copied"], n + 1)
                pe.wait_ge(S["wo_loaded"], 16 * (n // NB + 1))
                for f in range(FT):
                    last = pe.matmul(pm[:, 512:512 + P], wo[:, f, :], attnT[:, f, :], start=(f == 0),
                                     stop=(f == FT - 1))
                last.then_inc(S["wo_done"], 1)

            def ff_mean(n):
                pe.wait_ge(S["residual1"], n + 1)
                pe.matmul(pm[:, 512:512 + P], mean_w, xs2[:, 0:P], start=True, stop=True).then_inc(S["mean_done"], 1)

            def ff_var(n):
                pe.wait_ge(S["xc_squared"], n + 1)
                if runs(n - 1):
                    pe.wait_ge(S["hatted"], n)
                pe.matmul(pm[:, 0:P], xcsq[:, :], mean_w, start=True, stop=True)\
                  .then_inc(S["var_done"], 1)

            def spread_rstd(n):
                pe.wait_ge(S["refined"], ROOT_OPS * (n + 4))
                if runs(n - 1):
                    pe.wait_ge(S["x_ready"], NB + n)
                pe.matmul(pm[:, 0:P], root[:, 2 * HEADS:ROOTS].broadcast_to([P, P]), ident,
                          start=True, stop=True).then_inc(S["rstd_spread"], 1)

            def ff_up(n, dst):
                pe.wait_ge(S["xn2_ready"], n + 1)
                pe.wait_ge(S["w1_loaded"], 16 * (n // NB + 1))
                for half in range(2):
                    for t, (at, rows) in enumerate(FFT):
                        last = pe.matmul(dst[0:rows, 512 * half + t * P:512 * half + (t + 1) * P],
                                         w1[:, half * FF + at:half * FF + at + rows], xn2[:, :],
                                         start=True, stop=True)
                last.then_inc(S["up_done"], 1)

            def ff_down(n):
                pe.wait_ge(S["gated"], 3 * (n + 1))
                if runs(n + 1):
                    pe.wait_ge(S["refined"], ROOT_OPS * (n + 4) + 2)
                pe.wait_ge(S["w2_loaded"], 48 * (n // NB + 1))
                for t, (at, rows) in enumerate(FFT):
                    last = pe.matmul(pm[:, 0:P], w2[0:rows, t, :], hid[0:rows, t, :], start=(t == 0),
                                     stop=(t == 2))
                last.then_inc(S["down_done"], 1)

            def step(n, u):
                a, b, c = slots(u)
                if runs(n):
                    if isinstance(n, int) and n == 0:
                        pe.wait_ge(S["k_turned"], 3 * 2)
                    score(n, u, c)
                if runs(n - 1):
                    out_project(n - 1)
                if runs(n + 2):
                    project(n + 2, u, 1, b, "k_proj")
                if runs(n - 3):
                    ff_down(n - 3)
                if runs(n + 2):
                    if isinstance(n, int) and n == -1:
                        pe.wait_ge(S["q_turned"], 3)
                    if runs(n - 3):
                        pe.wait_ge(S["gated"], 3 * (n - 2))
                    project(n + 2, u, 0, a, "q_proj")
                if runs(n + 1):
                    if runs(n):
                        pe.wait_ge(S["masked"], n + 1)
                    else:
                        pe.wait_ge(S["k_turned"], 3)
                    project(n + 1, 1 - u, 2, c, "v_proj")
                if runs(n - 1):
                    ff_mean(n - 1)
                if runs(n):
                    pe.wait_ge(S["exped"], n + 1)
                    if runs(n + 2):
                        pe.wait_ge(S["k_turned"], 3 * (n + 3))
                    transpose_all(b, probs[:, :, :].rearrange("p h k -> p (h k)"), "pT_done")
                if runs(n + 1):
                    pe.wait_ge(S["q_scaled"], n + 2)
                    pe.wait_ge(S["v_copied"], n + 2)
                    transpose_all(c, rot[:, 1 - u, 0, :, :, :].rearrange("p h a d -> p (h a d)"), "qT_done")
                if runs(n + 1):
                    if runs(n + 2):
                        pe.wait_ge(S["q_turned"], 3 * (n + 3))
                    elif runs(n - 3):
                        pe.wait_ge(S["gated"], 3 * (n - 2))
                    pe.wait_ge(S["k_scaled"], n + 2)
                    transpose_all(a, rot[:, 1 - u, 1, :, :, :].rearrange("p h a d -> p (h a d)"), "kT_done")
                if runs(n - 2):
                    spread_rstd(n - 2)
                if runs(n):
                    attend(n, b)
                if runs(n - 2):
                    if runs(n + 1):
                        pe.wait_ge(S["kT_copied"], n + 2)
                    elif runs(n - 3):
                        pe.wait_ge(S["gated"], 3 * (n - 2))
                    ff_up(n - 2, a)
                if runs(n):
                    pe.wait_ge(S["normed"], n + 1)
                    if runs(n + 1):
                        pe.wait_ge(S["qT_copied"], n + 2)
                    transpose_all(c, attn[:, :, :].rearrange("p h d -> p (h d)"), "attnT_done")
                if runs(n - 1):
                    ff_var(n - 1)

            run(pe, step)

        @block.scalar
        def _(act):
            def stage(n, u):
                act.wait_ge(S["x_ready"], n + 1)
                if not (isinstance(n, int) and n == 0):
                    act.wait_ge(S["carried1"], n)
                x = slot(n)
                act.activation(xs1[0:64, u, 0:P], x[0:64, :], ACT.Copy)
                act.activation(xs1[64:P, u, 1:P + 1], x[64:P, :], ACT.Copy)
                act.activation(xs1[64:P, u, 0:1], carry1[64:P, bass.ds(n % BPB, 1)], ACT.Copy)\
                   .then_inc(S["staged1"], 1)
                act.activation(carry1[64:P, bass.ds(n % BPB + 1, 1)],
                               xT[64:P, bass.ds((n % NB) * P + P - 1, 1)], ACT.Copy).then_inc(S["carried1"], 1)

            def copy_k(n, u, src):
                if isinstance(n, int) and n == 0:
                    act.wait_ge(S["cleared_pool"], 2)
                act.wait_ge(S["kT_done"], n + 1)
                src = src[:, :].rearrange("p (f t) -> p f t", f=FT)
                for s in range(2):
                    rows = slice(64 * s, 64 * s + 64)
                    last = act.activation(kT[rows, u, :, s, WIN:WIN + P], src[rows, :, :], ACT.Copy)
                last.then_inc(S["kT_copied"], 1)

            def carry_k(n, u):
                act.wait_ge(S["kT_copied"], n + 1)
                for s in range(2):
                    rows = slice(64 * s, 64 * s + 64)
                    last = act.activation(kT[rows, 1 - u, :, s, 0:WIN], kT[rows, u, :, s, P:P + WIN], ACT.Copy)
                last.then_inc(S["k_carried"], 1)

            def square(n, k, src, proj, summed, done):
                if not (isinstance(n, int) and n == 0):
                    act.wait_ge(S[summed], n)
                for c in range(2):
                    act.wait_ge(S[proj], 2 * n + c + 1)
                    last = act.activation(squares[:, k, c * 512:(c + 1) * 512], src[:, c * 512:(c + 1) * 512],
                                          ACT.Square)
                last.then_inc(S[done], 1)

            def copy_v(n, u, src):
                if isinstance(n, int) and n == 0:
                    act.wait_ge(S["cleared_pool"], 1)
                else:
                    act.wait_ge(S["v_spread"], SPREADS * n)
                for c in range(2):
                    act.wait_ge(S["v_proj"], 2 * n + c + 1)
                    last = act.activation(vtok[:, u, :, 4 * c:4 * c + 4, :].rearrange("p s f d -> p f s d"),
                                          src[:, c * 512:(c + 1) * 512]
                                          .rearrange("p (f s d) -> p f s d", f=FT // 2, s=2), ACT.Copy)
                last.then_inc(S["v_copied"], 1)

            def exp(n):
                act.wait_ge(S["max_taken"], n + 1)
                act.activation(probs[:, :, :], sm[:, :, :], ACT.Exp, scale=SCORE_SCALE)\
                   .then_inc(S["exped"], 1)

            def copy_out(src, dst, waits, done, n):
                act.wait_ge(S[waits], n + 1)
                act.activation(dst[:, :, :].rearrange("p f t -> p (f t)"), src[:, :], ACT.Copy)\
                   .then_inc(S[done], 1)

            def ff_square(n):
                act.wait_ge(S["centered"], n + 1)
                act.activation(xcsq[:, :], xc[:, :], ACT.Square).then_inc(S["xc_squared"], 1)

            def ff_gelu(n, src):
                act.wait_ge(S["up_done"], n + 1)
                for t, (at, rows) in enumerate(FFT):
                    last = act.activation(gate[0:rows, t, :], src[0:rows, 512 + t * P:512 + (t + 1) * P],
                                          ACT.Gelu, bias=b1[0:rows, t, bass.ds(2 * (n // NB) + 1, 1)])
                last.then_inc(S["gelued"], 1)

            def step(n, u):
                a, b, c = slots(u)
                if runs(n):
                    if not (isinstance(n, int) and n == 0):
                        act.wait_ge(S["warmed_exp"], n)
                    act.activation(warm_exp[:, :], eps[:, 0:1], ACT.Exp).then_inc(S["warmed_exp"], 1)
                    carry_k(n, u)
                if runs(n + 2):
                    square(n + 2, 1, b, "k_proj", "k_summed", "k_squared")
                    square(n + 2, 0, a, "q_proj", "q_summed", "q_squared")
                if runs(n):
                    exp(n)
                if runs(n + 1):
                    copy_v(n + 1, 1 - u, c)
                if runs(n):
                    copy_out(b, pT, "pT_done", "pT_copied", n)
                if runs(n + 1):
                    copy_out(c, qT, "qT_done", "qT_copied", n + 1)
                if runs(n + 1):
                    copy_k(n + 1, 1 - u, a)
                if runs(n - 1):
                    ff_square(n - 1)
                if runs(n + 3):
                    stage(n + 3, 1 - u)
                if runs(n - 2):
                    if not (isinstance(n, int) and n == 2):
                        act.wait_ge(S["warmed"], n - 2)
                    act.activation(warm[:, :], eps[:, 0:1], ACT.Gelu).then_inc(S["warmed"], 1)
                    ff_gelu(n - 2, a)
                if runs(n):
                    copy_out(c, attnT, "attnT_done", "attnT_copied", n)

            act.wait_ge(S["tables_loaded"], 7 * 16)
            act.wait_ge(S["cleared"], 1)
            stage(0, 0)
            run(act, step)

        @block.vector
        def _(dve):
            def tables(n, u):
                dve.tensor_tensor(table[:, u, :, :].rearrange("p k d -> p (k d)"),
                                  rope[:, bass.ds(n % BPB, 1), :, :].rearrange("p a k d -> p (a k d)"),
                                  scales[:, bass.ds(n // NB, 1), :, :].rearrange("p a k d -> p (a k d)"),
                                  ALU.mult).then_inc(S["tabled"], 1)

            def turn(n, u, k, src, squared, turned, added):
                dve.wait_ge(S[squared], n + 1)
                if not (isinstance(n, int) and n == 0):
                    dve.wait_ge(S[added], n)
                cos = table[:, u, 2 * k, :]
                v = src[:, :].rearrange("p (h a d) -> p h a d", h=HEADS, a=2)
                dve.tensor_tensor(rot[:, u, k, :, :, :].rearrange("p h a d -> p h (a d)"),
                                  src[:, :].rearrange("p (h d) -> p h d", h=HEADS),
                                  bcast(cos, 1, HEADS), ALU.mult).then_inc(S[turned], 1)
                for a in range(2):
                    sin = table[:, u, 2 * k + 1, 32 * a:32 * a + 32]
                    dve.tensor_tensor(rot_sin[:, k, :, a, :], v[:, :, 1 - a, :], bcast(sin, 1, HEADS),
                                      ALU.mult).then_inc(S[turned], 1)

            def norm_square(n, k, folded, summed):
                dve.wait_ge(S[folded], n + 1)
                dve.tensor_reduce(ss[:, k, :], squares[:, k, :].rearrange("p (h a d) -> p h a d", h=HEADS, a=2)
                                  [:, :, 0, :], AX.X, ALU.add).then_inc(S[summed], 1)

            def find_roots(n):
                before = ROOT_OPS * (n + 1)
                if runs(n + 1):
                    dve.wait_ge(S["q_summed"], n + 2)
                    dve.wait_ge(S["k_summed"], n + 2)
                    dve.tensor_scalar(minus_half[:, 0:2 * HEADS], ss[:, :, :].rearrange("p k h -> p (k h)"),
                                      1e-24, -0.5, ALU.max, ALU.mult)\
                       .then_inc(S["refined"], 1 if runs(n - 2) else 2)
                if runs(n - 2):
                    dve.wait_ge(S["var_done"], n - 1)
                    dve.tensor_scalar(minus_half[:, 2 * HEADS:ROOTS], pm[:, 0:1], 1e-5, -0.5, ALU.add, ALU.mult)\
                       .then_inc(S["refined"], 1 if runs(n + 1) else 2)
                dve.wait_ge(S["refined"], before + 2)
                if runs(n):
                    dve.wait_ge(S["q_scaled"], n + 1)
                if runs(n - 3):
                    dve.wait_ge(S["rstd_spread"], n - 2)
                dve.tensor_scalar(root[:, :].bitcast(I32), minus_half[:, :].bitcast(I32), -0.5, GUESS,
                                  ALU.mult, ALU.add).then_inc(S["refined"], 1)
                for i in range(NEWTON):
                    dve.wait_ge(S["refined"], before + 3 + 3 * i)
                    dve.tensor_tensor(root_t[:, :], minus_half[:, :], root[:, :], ALU.mult)\
                       .then_inc(S["refined"], 1)
                    dve.wait_ge(S["refined"], before + 4 + 3 * i)
                    dve.tensor_tensor(root_t[:, :], root_t[:, :], root[:, :], ALU.mult)\
                       .then_inc(S["refined"], 1)
                    dve.wait_ge(S["refined"], before + 5 + 3 * i)
                    dve.scalar_tensor_tensor(out=root[:, :], in0=root_t[:, :], scalar=1.5, in1=root[:, :],
                                             op0=ALU.add, op1=ALU.mult).then_inc(S["refined"], 1)

            def mask(n, u, src):
                dve.wait_ge(S["scores_done"], n + 1)
                m = window[:, bass.ds((n // 2) % 4, 1), :].rearrange("p a k -> p (a k)") if u == 0 \
                    else window[:, 1, :]
                dve.tensor_tensor(sm[:, :, :], src[:, :].rearrange("p (h k) -> p h k", h=HEADS),
                                  bcast(m, 1, HEADS), ALU.add).then_inc(S["masked"], 1)
                dve.wait_ge(S["masked"], n + 1)
                dve.tensor_reduce(rowmax[:, :], sm[:, :, :], AX.X, ALU.max).then_inc(S["maxed"], 1)

            def sums(n):
                dve.wait_ge(S["exped"], n + 1)
                dve.tensor_reduce(rowsum[:, :], probs[:, :, :], AX.X, ALU.add).then_inc(S["summed"], 1)
                dve.wait_ge(S["summed"], n + 1)
                dve.reciprocal(rinv[:, :], rowsum[:, :]).then_inc(S["inverted"], 1)

            def normalise(n, src):
                dve.wait_ge(S["vwin_free"], n + 2)
                dve.wait_ge(S["inverted"], n + 1)
                dve.tensor_tensor(attn[:, :, :], src[:, :].rearrange("p (h d) -> p h d", h=HEADS),
                                  bcast(rinv[:, :], 2, DH), ALU.mult).then_inc(S["normed"], 1)

            def residual1(n):
                dve.wait_ge(S["wo_done"], n + 1)
                y, x = pm[:, 512:512 + P], slot(n)
                dve.tensor_tensor(xs2[0:64, 0:P], y[0:64, :], x[0:64, :], ALU.add)
                dve.tensor_tensor(xs2[64:P, 1:P + 1], y[64:P, :], x[64:P, :], ALU.add).then_inc(S["shifted2"], 1)
                if not (isinstance(n, int) and n == 0):
                    dve.wait_ge(S["carried2"], n)
                dve.tensor_copy(xs2[64:P, 0:1], carry2[64:P, bass.ds(n % BPB, 1)])
                dve.wait_ge(S["shifted2"], n + 1)
                dve.tensor_tensor(x, y, x, ALU.add).then_inc(S["residual1"], 1)
                dve.tensor_copy(carry2[64:P, bass.ds(n % BPB + 1, 1)], xs2[64:P, P:P + 1])\
                   .then_inc(S["carried2"], 1)

            def center(n):
                dve.wait_ge(S["mean_done"], n + 1)
                dve.tensor_tensor(xc[:, :], xs2[:, 0:P], pm[:, 512:512 + P], ALU.subtract)\
                   .then_inc(S["centered"], 1)

            def ff_norm(n):
                dve.wait_ge(S["rstd_spread"], n + 1)
                dve.tensor_tensor(xhat[:, :], xc[:, :], pm[:, 0:P], ALU.mult).then_inc(S["hatted"], 1)
                dve.wait_ge(S["hatted"], n + 1)
                layer = n // NB
                dve.tensor_scalar(xn2[:, :], xhat[:, :], cols[:, 0, bass.ds(layer, 1)],
                                  cols[:, 1, bass.ds(layer, 1)], ALU.mult, ALU.add)\
                   .then_inc(S["xn2_ready"], 1)

            def ff_gate(n, src):
                dve.wait_ge(S["gelued"], n + 1)
                for t, (at, rows) in enumerate(FFT):
                    dve.scalar_tensor_tensor(out=hid[0:rows, t, :], in0=src[0:rows, t * P:(t + 1) * P],
                                             scalar=b1[0:rows, t, bass.ds(2 * (n // NB), 1)],
                                             in1=gate[0:rows, t, :], op0=ALU.add, op1=ALU.mult)\
                       .then_inc(S["gated"], 1)

            def residual2(n):
                dve.wait_ge(S["down_done"], n + 1)
                dve.wait_ge(S["residual1"], n + 1)
                dve.scalar_tensor_tensor(out=slot(n), in0=pm[:, 0:P], scalar=cols[:, 2, bass.ds(n // NB, 1)],
                                         in1=slot(n), op0=ALU.add, op1=ALU.add).then_inc(S["x_ready"], 1)

            def step(n, u):
                a, b, c = slots(u)
                if runs(n + 2):
                    tables(n + 2, u)
                if runs(n - 3):
                    ff_gate(n - 3, a)
                if runs(n + 1) or runs(n - 2):
                    find_roots(n)
                if runs(n):
                    mask(n, u, c)
                if runs(n - 1):
                    residual1(n - 1)
                if runs(n + 2):
                    dve.wait_ge(S["tabled"], n + 3)
                    turn(n + 2, u, 1, b, "k_squared", "k_turned", "k_added")
                    turn(n + 2, u, 0, a, "q_squared", "q_turned", "q_added")
                if runs(n - 3):
                    residual2(n - 3)
                if runs(n):
                    sums(n)
                if runs(n - 2):
                    ff_norm(n - 2)
                if runs(n - 1):
                    center(n - 1)
                if runs(n + 2):
                    norm_square(n + 2, 1, "k_folded", "k_summed")
                if runs(n):
                    normalise(n, b)
                if runs(n + 2):
                    norm_square(n + 2, 0, "q_folded", "q_summed")

            dve.memset(xs1[:, :, :], 0.0)
            dve.memset(minus_half[:, :], -0.5)
            dve.memset(carry1[:, :], 0.0).then_inc(S["cleared"], 1)
            dve.memset(carry2[:, :], 0.0).then_inc(S["x_ready"], NB)
            dve.wait_ge(S["tables_loaded"], 7 * 16)
            run(dve, step)

        @block.gpsimd
        def _(pool):
            pool.memset(vtok[:, :, :, :, :], 0.0).then_inc(S["cleared_pool"], 1)
            pool.memset(kT[:, :, :, :, :], 0.0).then_inc(S["cleared_pool"], 1)
            pool.memset(vwin[:, :, :, :, :], 0.0).then_inc(S["vwin_free"], 1)

            def add(n, u, k, turned, added):
                pool.wait_ge(S[turned], 3 * (n + 1))
                r = rot[:, u, k, :, :, :].rearrange("p h a d -> p h (a d)")
                pool.tensor_tensor(r, r, rot_sin[:, k, :, :, :].rearrange("p h a d -> p h (a d)"), ALU.add)\
                    .then_inc(S[added], 1)

            def fold(n, k, squared, folded):
                pool.wait_ge(S[squared], n + 1)
                halves = squares[:, k, :].rearrange("p (h a d) -> p h a d", h=HEADS, a=2)
                pool.tensor_tensor(halves[:, :, 0, :], halves[:, :, 0, :], halves[:, :, 1, :], ALU.add)\
                    .then_inc(S[folded], 1)

            def scale(n, u, k, added, scaled):
                pool.wait_ge(S[added], n + 1)
                pool.wait_ge(S["refined"], ROOT_OPS * (n + 1))
                r = rot[:, u, k, :, :, :].rearrange("p h a d -> p h (a d)")
                pool.tensor_tensor(r, r, bcast(root[:, k * HEADS:(k + 1) * HEADS], 2, DH), ALU.mult)\
                    .then_inc(S[scaled], 1)

            def take_max(n):
                pool.wait_ge(S["maxed"], n + 1)
                pool.tensor_tensor(sm[:, :, :], sm[:, :, :], bcast(rowmax[:, :], 2, 2 * WIN), ALU.subtract)\
                    .then_inc(S["max_taken"], 1)

            def step(n, u):
                if runs(n + 1):
                    scale(n + 1, 1 - u, 1, "k_added", "k_scaled")
                if runs(n):
                    take_max(n)
                if runs(n + 1):
                    scale(n + 1, 1 - u, 0, "q_added", "q_scaled")
                if runs(n + 2):
                    fold(n + 2, 1, "k_squared", "k_folded")
                    fold(n + 2, 0, "q_squared", "q_folded")
                    add(n + 2, u, 1, "k_turned", "k_added")
                    add(n + 2, u, 0, "q_turned", "q_added")

            run(pool, step)


def last_norm(nc, x1, xT, ident, eps, out):
    with ExitStack() as ctx:
        y = ctx.enter_context(nc.sbuf_tensor("y", [P, NB, P], F32))
        ps = ctx.enter_context(nc.psum_tensor("ps_last", [P, NB * P], F32))
        turned = ctx.enter_context(nc.semaphore("turned"))
        added = ctx.enter_context(nc.semaphore("added"))
        stored = ctx.enter_context(nc.semaphore("stored"))
        norm = Norm(nc, ctx, "ln_last", eps[:, 0:1])
        block = ctx.enter_context(nc.Block())

        def part(tile):
            return lambda q: tile[:, q * PB:(q + 1) * PB, :]

        @block.tensor
        def _(pe):
            for q in range(PARTS):
                for n in range(q * PB, (q + 1) * PB):
                    last = pe.transpose(ps[:, n * P:(n + 1) * P], xT[:, n * P:(n + 1) * P], ident)
                last.then_inc(turned, 1)

        @block.scalar
        def _(act):
            norm.scalar(act, 0, part(y))

        @block.vector
        def _(dve):
            norm.vector(dve, 0, lambda q: ps[:, q * PB * P:(q + 1) * PB * P].rearrange("p (n d) -> p n d", n=PB),
                        part(y), lambda q: dve.wait_ge(turned, q + 1))

        @block.gpsimd
        def _(pool):
            for q in range(PARTS):
                pool.wait_ge(norm.done, q + 1)
                pool.tensor_tensor(part(y)(q), part(y)(q), part(x1)(q), ALU.add).then_inc(added, 1)

        @block.sync
        def _(sp):
            for q in range(PARTS):
                sp.wait_ge(added, q + 1)
                sp.dma_start(out[q * PB * P:(q + 1) * PB * P, :].rearrange("(n p) d -> p n d", p=P), part(y)(q))\
                  .then_inc(stored, 16)
            sp.wait_ge(stored, 16 * PARTS)


def _constants(np):
    eye = np.eye(P)
    i = np.arange(P)
    causal = (i[:, None] <= i[None, :]).astype(float)
    blocks = (i[:, None] // LD == i[None, :] // LD).astype(float)
    square = np.stack([eye, np.full((P, P), 1.0 / P), causal, blocks], 1).astype(np.float32)
    head = (i[:, None] // LD == np.arange(LH)[None, :]).astype(np.float32)
    cols = (np.arange(P // LG)[None, :] // LD == np.arange(LGH)[:, None]).reshape(-1).astype(np.float32)
    q = (i % WIN)[:, None]
    k = np.arange(2 * WIN)[None, :]
    allowed = (q <= k) & (k <= q + WIN)
    first = allowed & ((i[:, None] >= WIN) | (k >= WIN))
    window = np.where(np.stack([first, allowed, allowed, allowed], 1), 0.0, MASKED).astype(np.float32)
    half = np.arange(0, DH, 2, dtype=np.float32)
    inv_freq = np.float32(1.0) / np.float32(10000.0) ** (half / np.float32(DH))
    t = np.arange(SEQ, dtype=np.float32)
    freqs = t[:, None] * inv_freq[None, :]
    base = (half + np.float32(0.4 * DH)) / np.float32(1.4 * DH)
    power = (t - SEQ // 2) / np.float32(WIN // 2)
    scale = base[None, :] ** power[:, None]
    cos, sin = np.cos(freqs), np.sin(freqs)
    both = lambda a, b: np.concatenate([a, b], -1)
    parts = [both(cos * scale, cos * scale), both(-sin * scale, sin * scale),
             both(cos / scale, cos / scale), both(-sin / scale, sin / scale)]
    rope = np.stack(parts, 1).reshape(BPB, P, 4, DH).transpose(1, 0, 2, 3).astype(np.float32)
    return square, head, cols, window, np.ascontiguousarray(rope)


def kernel(L0_attn_X, L0_attn_Wq, L0_attn_Wv, L0_attn_q_norm_w, L0_attn_v_norm_w, L0_ffn_Wqkv,
           L0_ffn_q_scale, L0_ffn_k_scale, L0_ffn_Wo, L0_ffn_ln_g, L0_ffn_ln_b, L0_ffn_W1, L0_ffn_b1,
           L0_ffn_W2, L0_ffn_b2):
    import numpy as np
    import concourse.bacc as bacc
    from concourse.bass_utils import run_bass_kernel_spmd

    a = np.asarray
    square, head, head_cols, window, rope = _constants(np)
    qs, ks = a(L0_ffn_q_scale), a(L0_ffn_k_scale)
    laid = {
        "x": a(L0_attn_X).reshape(BATCH * SEQ, P),
        "wqv": np.concatenate([a(L0_attn_Wq).T, a(L0_attn_Wv).T], 1),
        "lin_w": np.concatenate([a(L0_attn_q_norm_w).reshape(-1), a(L0_attn_v_norm_w).reshape(-1)]),
        "wqkv": a(L0_ffn_Wqkv),
        "scales": np.stack([qs, np.roll(qs, DH // 2, 1), ks, np.roll(ks, DH // 2, 1)], 1),
        "wo": a(L0_ffn_Wo),
        "w1": a(L0_ffn_W1),
        "b1": a(L0_ffn_b1).reshape(LAYERS, 2, FF).transpose(2, 0, 1).reshape(FF, 2 * LAYERS),
        "w2": a(L0_ffn_W2),
        "cols": np.stack([a(L0_ffn_ln_g).T, a(L0_ffn_ln_b).T, a(L0_ffn_b2).T], 1),
        "square": square, "head": head, "head_cols": head_cols, "window": window, "rope": rope,
    }
    laid = {f"in_{name}": np.ascontiguousarray(v) for name, v in laid.items()}
    nc = bacc.Bacc("TRN2", target_bir_lowering=False, num_devices=1)
    args = [nc.dram_tensor(name, v.shape, mybir.dt.from_np(v.dtype), kind="ExternalInput").ap()
            for name, v in laid.items()]
    out = nc.dram_tensor("out_x", (BATCH * SEQ, P), F32, kind="ExternalOutput").ap()
    build(nc, *args, out)
    r = run_bass_kernel_spmd(nc, [laid], core_ids=[0])
    return r.results[0]["out_x"].reshape(BATCH, SEQ, P)
```
